# Optimizing a Trainium2 kernel written in Bass

```python
import numpy as np
import jax
import jax.numpy as jnp

def _softmax(x, axis=-1):
    return jax.nn.softmax(x, axis=axis)

def _gelu(x):
    return jax.nn.gelu(x, approximate=True)

def _silu(x):
    return jax.nn.silu(x)

def _sigmoid(x):
    return jax.nn.sigmoid(x)

def _layernorm(x, axis=-1, eps=1e-05):
    m = jnp.mean(x, axis=axis, keepdims=True)
    v = jnp.var(x, axis=axis, keepdims=True)
    return (x - m) / jnp.sqrt(v + eps)

def _scatter_add(tgt, idx, src, axis=0):
    return tgt.at[idx].add(src)

def _segment_sum(src, seg, n):
    return jax.ops.segment_sum(src, seg, n)
kernel_name = 'mk_adj_preln_d1_adj_r2_c89a44'

def setup_inputs(seed: int=0):
    np.random.seed(seed)
    _w = jnp.asarray

    def _rec_inputs():
        import jax
        import jax.numpy as jnp
        _gk = jax.random.key(seed)
        x = -0.001547 + 1.001 * jax.random.normal(jax.random.fold_in(_gk, 1), (128, 128, 128), jnp.float32)
        _a = jax.random.bernoulli(jax.random.fold_in(_gk, 2), 0.125, (128, 128, 128))
        _a = jnp.logical_or(_a, jnp.eye(128, dtype=bool))
        adj = _a.astype(jnp.int32)
        _nm = jnp.ones((128, 128), dtype=bool)
        nodemask = jnp.where(_nm, 1.0, 0.0).astype(jnp.float32)
        return (x, adj, nodemask)
    x, adj, nodemask = _rec_inputs()

    def _L0_gnn_setup():
        import jax, jax.numpy as jnp
        import numpy as np
        D_MODEL = 128
        NUM_REL = 40

        def _direction(x, W, Wg, b, bg, adj, rel_ids):
            h = x @ W.T
            g = h @ Wg.T
            vals = (h[:, :, None, :] + b) * jax.nn.sigmoid(g[:, :, None, :] + bg)
            onehot = (adj[..., None] == rel_ids).astype(h.dtype)
            return jnp.einsum('bnmr,bmrd->bnd', onehot, vals)
        key = jax.random.key(seed)
        ks = jax.random.split(key, 16)
        B, N, d = (2, 256, D_MODEL)
        s = 0.02
        inp = {'node': jax.random.normal(ks[0], (B, N, d), dtype=jnp.float32), 'node_mask': jnp.ones((B, N), dtype=jnp.float32), 'adj_mat': jax.random.randint(ks[1], (B, N, N), 0, 41, dtype=jnp.int32), 'W_fwd': jax.random.normal(ks[2], (d, d), dtype=jnp.float32) * s, 'W_bwd': jax.random.normal(ks[3], (d, d), dtype=jnp.float32) * s, 'W_loop': jax.random.normal(ks[4], (d, d), dtype=jnp.float32) * s, 'Wg_fwd': jax.random.normal(ks[5], (d, d), dtype=jnp.float32) * s, 'Wg_bwd': jax.random.normal(ks[6], (d, d), dtype=jnp.float32) * s, 'Wg_loop': jax.random.normal(ks[7], (d, d), dtype=jnp.float32) * s, 'b_fwd': jax.random.normal(ks[8], (NUM_REL - 1, d), dtype=jnp.float32) * s, 'b_bwd': jax.random.normal(ks[9], (NUM_REL - 1, d), dtype=jnp.float32) * s, 'b_loop': jax.random.normal(ks[10], (1, d), dtype=jnp.float32) * s, 'bg_fwd': jax.random.normal(ks[11], (NUM_REL - 1, d), dtype=jnp.float32) * s, 'bg_bwd': jax.random.normal(ks[12], (NUM_REL - 1, d), dtype=jnp.float32) * s, 'bg_loop': jax.random.normal(ks[13], (1, d), dtype=jnp.float32) * s}
        return inp
    _L0_gnn_all = _L0_gnn_setup()
    _L0_gnn_in = {k: v for k, v in _L0_gnn_all.items() if k in ('W_fwd', 'W_bwd', 'W_loop', 'Wg_fwd', 'Wg_bwd', 'Wg_loop', 'b_fwd', 'b_bwd', 'b_loop', 'bg_fwd', 'bg_bwd', 'bg_loop')}
    del _L0_gnn_all
    return {'x': x, 'adj': adj, 'nodemask': nodemask, 'L0_gnn_W_fwd': _L0_gnn_in['W_fwd'], 'L0_gnn_W_bwd': _L0_gnn_in['W_bwd'], 'L0_gnn_W_loop': _L0_gnn_in['W_loop'], 'L0_gnn_Wg_fwd': _L0_gnn_in['Wg_fwd'], 'L0_gnn_Wg_bwd': _L0_gnn_in['Wg_bwd'], 'L0_gnn_Wg_loop': _L0_gnn_in['Wg_loop'], 'L0_gnn_b_fwd': _L0_gnn_in['b_fwd'], 'L0_gnn_b_bwd': _L0_gnn_in['b_bwd'], 'L0_gnn_b_loop': _L0_gnn_in['b_loop'], 'L0_gnn_bg_fwd': _L0_gnn_in['bg_fwd'], 'L0_gnn_bg_bwd': _L0_gnn_in['bg_bwd'], 'L0_gnn_bg_loop': _L0_gnn_in['bg_loop']}

def reference(x, adj, nodemask, L0_gnn_W_fwd, L0_gnn_W_bwd, L0_gnn_W_loop, L0_gnn_Wg_fwd, L0_gnn_Wg_bwd, L0_gnn_Wg_loop, L0_gnn_b_fwd, L0_gnn_b_bwd, L0_gnn_b_loop, L0_gnn_bg_fwd, L0_gnn_bg_bwd, L0_gnn_bg_loop):
    import jax
    import jax.numpy as jnp

    def _L0_gnn_ref(node, node_mask, adj_mat, W_fwd, W_bwd, W_loop, Wg_fwd, Wg_bwd, Wg_loop, b_fwd, b_bwd, b_loop, bg_fwd, bg_bwd, bg_loop):
        import jax, jax.numpy as jnp
        import numpy as np
        D_MODEL = 128
        NUM_REL = 40

        def _direction(x, W, Wg, b, bg, adj, rel_ids):
            h = x @ W.T
            g = h @ Wg.T
            vals = (h[:, :, None, :] + b) * jax.nn.sigmoid(g[:, :, None, :] + bg)
            onehot = (adj[..., None] == rel_ids).astype(h.dtype)
            return jnp.einsum('bnmr,bmrd->bnd', onehot, vals)
        rels = jnp.arange(2, NUM_REL + 1, dtype=adj_mat.dtype)
        rel1 = jnp.array([1], dtype=adj_mat.dtype)
        adj_t = jnp.swapaxes(adj_mat, -1, -2)
        out = _direction(node, W_fwd, Wg_fwd, b_fwd, bg_fwd, adj_mat, rels)
        out = out + _direction(node, W_bwd, Wg_bwd, b_bwd, bg_bwd, adj_t, rels)
        out = out + _direction(node, W_loop, Wg_loop, b_loop, bg_loop, adj_t, rel1)
        return jax.nn.relu(out)
    h = jnp.maximum(_layernorm(x, axis=-1), 0.0)
    x = x + _L0_gnn_ref(h, nodemask, adj, L0_gnn_W_fwd, L0_gnn_W_bwd, L0_gnn_W_loop, L0_gnn_Wg_fwd, L0_gnn_Wg_bwd, L0_gnn_Wg_loop, L0_gnn_b_fwd, L0_gnn_b_bwd, L0_gnn_b_loop, L0_gnn_bg_fwd, L0_gnn_bg_bwd, L0_gnn_bg_loop)
    return x

_drawn_inputs = setup_inputs


def setup_inputs(seed=0):
    import zlib

    import numpy as np

    out = dict(_drawn_inputs(seed))
    spreads = {}
    factors = {'L0_gnn_Wg_loop': 8.0, 'L0_gnn_bg_loop': 8.0}
    for name, (base, spread) in spreads.items():
        noise = np.random.default_rng([zlib.crc32(name.encode()), seed]).standard_normal(out[name].shape)
        drawn = base * np.exp(spread * noise) if base else spread * noise
        out[name] = jnp.asarray(drawn.astype(out[name].dtype))
    for name, factor in factors.items():
        out[name] = (out[name] * factor).astype(out[name].dtype)
    return out
```

```python
from contextlib import ExitStack

import numpy as np
import concourse.bass as bass
from concourse import mybir

FP32, BF16, INT32 = mybir.dt.float32, mybir.dt.bfloat16, mybir.dt.int32
ALU = mybir.AluOpType
ACT = mybir.ActivationFunctionType
AX = mybir.AxisListType

EPS = 1e-5
GROUP = 4
CHUNK = 2
UNROLL = 4
REL_BLOCK = 3


def build(nc, x, adj, W_fwd, W_bwd, W_loop, Wg_fwd, Wg_bwd, Wg_loop,
          b_fwd, b_bwd, b_loop, bg_fwd, bg_bwd, bg_loop, out):
    B, N, D = x.shape
    NREL = b_fwd.shape[0]
    assert N == 128 and D == 128 and B % (GROUP * CHUNK) == 0 and NREL % REL_BLOCK == 0
    GROUPS = B // GROUP
    CHUNKS = GROUPS // CHUNK
    GC = GROUP * D
    CG = GROUP * CHUNK
    CC = CG * D

    STATS, NORM, HT, PROD = 6, 3, 2, 1
    LOOP_FROM = 2
    LOOP_TO = LOOP_FROM + (GROUPS - STATS - LOOP_FROM) // UNROLL * UNROLL
    assert LOOP_TO > LOOP_FROM
    LOAD_AHEAD = 6

    ctx = ExitStack()
    with ctx:
        def sb(name, shape, dt=FP32):
            return ctx.enter_context(nc.sbuf_tensor(name, shape, dt))

        def sem(name):
            return ctx.enter_context(nc.semaphore(name))

        SIDE = max(B * D, 2 * NREL * D + 36 * D)
        x_all = sb("x_all", [128, SIDE])
        adj_all = sb("adj_all", [128, SIDE], INT32)
        xn = sb("xn", [128, 2, GC])
        hT = sb("hT", [128, 2, GC])
        gate = sb("gate", [128, 2, GC])
        vals = sb("vals", [128, 2, GC])
        mask = sb("mask", [128, 2, GROUP * N])
        stats = sb("stats", [128, 2, CG, 6])
        sum_neg = sb("sum_neg", [128, CG])
        diff = sb("diff", [128, CG])
        diff_sq = sb("diff_sq", [128, CG])
        squares = sb("squares", [128, CG])
        var4 = sb("var4", [128, CG])
        mean_neg = sb("mean_neg", [128, 2, CG])
        var_eps = sb("var_eps", [128, 2, CG])
        rstd = sb("rstd", [128, 2, CG])
        shift = sb("shift", [128, 2, CG])
        minus_half = sb("minus_half", [128, CG])
        minus_one = sb("minus_one", [128, 1])
        ident = sb("ident", [128, 128])
        ones = sb("ones", [128, 1])
        w_raw = sb("w_raw", [128, 2, 128])
        w_gT = sb("w_gT", [128, 128])
        w_loop = sb("w_loop", [128, 2, D])
        ones_b = sb("ones_b", [128, 128], BF16)
        bias_rows = sb("bias_rows", [128, 2, GC], BF16)
        bias_in = sb("bias_in", [3, 2, D])
        part = [sb(f"part{n}", [3, 2 * D], BF16) for n in range(3)]
        rest = [sb(f"rest{n}", [3, 2 * D]) for n in range(2)]
        mix = [sb(f"mix{n}", [3, 2 * D]) for n in range(2)]
        junk = sb("junk", [128, CC], BF16)
        high = sb("high", [128, CHUNKS])
        high_sum = sb("high_sum", [1, 1])
        flag = sb("flag", [1, 1], INT32)

        bank = [ctx.enter_context(nc.psum_tensor(f"bank{n}", [128, 512], FP32)) for n in range(8)]
        hT_ps, gate_ps, val_ps, agg_ps = bank[0:2], bank[2:4], bank[4:6], bank[6:8]

        x_loaded = [sem(f"x_loaded{n}") for n in range(2)]
        adj_loaded = [sem(f"adj_loaded{n}") for n in range(2)]
        w_loaded = sem("w_loaded")
        bias_loaded = sem("bias_loaded")
        const_ready = sem("const_ready")
        half_ready = sem("half_ready")
        minus_ready = sem("minus_ready")
        w_turned = sem("w_turned")
        w_copied = sem("w_copied")
        bias_step = sem("bias_step")
        stat_step = sem("stat_step")
        var_step = sem("var_step")
        stats_ready = sem("stats_ready")
        rstd_ready = sem("rstd_ready")
        coef_ready = sem("coef_ready")
        normed = sem("normed")
        turned = sem("turned")
        hT_ready = sem("hT_ready")
        gate_prod = sem("gate_prod")
        val_prod = sem("val_prod")
        gate_ready = sem("gate_ready")
        vals_ready = sem("vals_ready")
        mask_ready = sem("mask_ready")
        summed = sem("summed")
        out_ready = sem("out_ready")
        stored = sem("stored")
        high_ready = sem("high_ready")
        high_total = sem("high_total")
        flag_step = sem("flag_step")
        flag_ready = sem("flag_ready")

        adj_f32 = adj_all[:, :].bitcast(FP32)
        TABLE = NREL * D
        room = {"x": 0, "a": 0}

        def view(side, cols):
            base = x_all[:, :] if side == "x" else adj_f32
            at = room[side]
            room[side] += cols
            assert room[side] <= SIDE
            return base[:, at:at + cols]

        DIRS = (("fwd", W_fwd, Wg_fwd), ("bwd", W_bwd, Wg_bwd))
        b_tab = [view("x", TABLE) for _ in DIRS]
        bg_tab = [view("a", TABLE) for _ in DIRS]
        RB = REL_BLOCK * D
        g_x, g_xn, g_hT, g_adjf, g_adjT, g_out = (view("x", D) for _ in range(6))
        g_vals = [view("x", RB) for _ in range(2)] + [view("x", D)]
        g_P = view("x", 3 * D)
        b_loop_tab = view("x", D)
        g_W = view("x", 3 * D)
        g_gatein = [view("a", RB) for _ in range(2)] + [view("a", D)]
        g_gate = [view("a", RB) for _ in range(2)] + [view("a", D)]
        g_mask = [view("a", RB) for _ in range(2)] + [view("a", D)]
        g_G = view("a", 3 * D)
        bg_loop_tab = view("a", D)
        g_C = view("a", 3 * D)
        g_wraw = view("a", 4 * D)
        g_wgT = view("a", 2 * D)
        g_adj = sb("g_adj", [128, N], INT32)
        g_stats = sb("g_stats", [128, 6])
        g_moments = sb("g_moments", [128, 2])
        g_var = sb("g_var", [128, 1])
        g_rstd = sb("g_rstd", [128, 1])
        rel_int = sb("rel_int", [128, NREL], INT32)
        rel_id = sb("rel_id", [128, NREL])
        BLOCKS = NREL // REL_BLOCK
        UNITS = 2 * BLOCKS

        tab_loaded = sem("tab_loaded")
        rel_made = sem("rel_made")
        g_setup = sem("g_setup")
        g_w_turned = sem("g_w_turned")
        g_loaded = sem("g_loaded")
        g_stat_step = sem("g_stat_step")
        g_rstd_ready = sem("g_rstd_ready")
        g_normed = sem("g_normed")
        g_turned = sem("g_turned")
        g_hT_ready = sem("g_hT_ready")
        g_prod = sem("g_prod")
        g_PG = sem("g_PG")
        g_in_ready = sem("g_in_ready")
        g_gate_ready = sem("g_gate_ready")
        g_val_step = sem("g_val_step")
        g_vals_ready = sem("g_vals_ready")
        g_summed = sem("g_summed")
        l_in_ready = sem("l_in_ready")
        l_gate_ready = sem("l_gate_ready")
        l_val_step = sem("l_val_step")
        l_vals_ready = sem("l_vals_ready")
        g_out_ready = sem("g_out_ready")
        g_stored = sem("g_stored")

        def live(g):
            return not isinstance(g, int) or 0 <= g < GROUPS

        def late(g, slots=2):
            return not isinstance(g, int) or g >= slots

        def steps(eng, step, first, last):
            for t in range(first, LOOP_FROM):
                step(t, t // CHUNK, t % UNROLL)
            with eng.Fori(LOOP_FROM // CHUNK, (LOOP_TO - UNROLL) // CHUNK + 1, UNROLL // CHUNK) as c:
                for j in range(UNROLL):
                    step(c * CHUNK + j, c + j // CHUNK, (LOOP_FROM + j) % UNROLL)
            for t in range(LOOP_TO, last):
                step(t, t // CHUNK, t % UNROLL)

        def chunk_after(c, phase, ahead):
            return c + (phase % CHUNK + ahead) // CHUNK

        def arrived(eng, loaded, c, phase):
            p = phase // CHUNK % 2
            eng.wait_ge(loaded[p], (c - p) * 8 + 16)

        block = ctx.enter_context(nc.Block())

        @block.sync
        def _(sp):
            def places(c):
                if isinstance(c, int):
                    return c * CG, c * CC
                return sp.snap(c * CG), sp.snap(c * CC)

            def load(c, p):
                at, col = places(c)
                if not isinstance(c, int) or c >= 2:
                    sp.wait_ge(x_loaded[p], (c - p) * 8)
                    sp.wait_ge(adj_loaded[p], (c - p) * 8)
                sp.dma_start(x_all[:, bass.ds(col, CC)].rearrange("p (b d) -> p b d", b=CG),
                             x[bass.ds(at, CG), :, :].rearrange("b n d -> n b d")).then_inc(x_loaded[p], 16)
                sp.dma_start(adj_all[:, bass.ds(col, CC)].rearrange("p (b n) -> p b n", b=CG),
                             adj[bass.ds(at, CG), :, :].rearrange("b n m -> n b m")
                             ).then_inc(adj_loaded[p], 16)

            def store(c):
                at, col = places(c)
                sp.wait_ge(out_ready, c * CHUNK + CHUNK)
                sp.dma_start(out[bass.ds(at, CG), :, :].rearrange("b n d -> n b d"),
                             x_all[:, bass.ds(col, CC)].rearrange("p (b d) -> p b d", b=CG)
                             ).then_inc(stored, 16)

            ahead = min(LOAD_AHEAD, CHUNKS)
            for c in range(ahead):
                load(c, c % 2)
            even = (CHUNKS - ahead) // 2 * 2
            if even:
                with sp.Fori(ahead, ahead + even - 1, 2) as c:
                    for j in range(2):
                        load(c + j, (ahead + j) % 2)
                        store(c + j - ahead)
            for c in range(even, CHUNKS):
                store(c)
            sp.wait_ge(stored, 16 * CHUNKS)

            sp.wait_ge(flag_ready, 1)
            with sp.If(sp.value_load(flag[0:1, 0:1], min_val=0, max_val=1) != 0):
                for d, (b_, bg_) in enumerate(((b_fwd, bg_fwd), (b_bwd, bg_bwd))):
                    sp.dma_start(b_tab[d], b_.rearrange("(o r) d -> o (r d)", o=1).to_broadcast([128, TABLE])
                                 ).then_inc(tab_loaded, 16)
                    sp.dma_start(bg_tab[d], bg_.rearrange("(o r) d -> o (r d)", o=1).to_broadcast([128, TABLE])
                                 ).then_inc(tab_loaded, 16)
                sp.dma_start(b_loop_tab, b_loop.to_broadcast([128, D])).then_inc(tab_loaded, 16)
                sp.dma_start(bg_loop_tab, bg_loop.to_broadcast([128, D])).then_inc(tab_loaded, 16)
                for d, (_, W, Wg) in enumerate(DIRS):
                    sp.dma_start(g_wraw[:, 2 * d * D:2 * d * D + D], W).then_inc(tab_loaded, 16)
                    sp.dma_start(g_wraw[:, 2 * d * D + D:2 * d * D + 2 * D], Wg).then_inc(tab_loaded, 16)
                sp.sem_inc(g_stored, 16)
                with sp.Fori(0, B) as b:
                    sp.wait_ge(g_stored, b * 16 + 16)
                    sp.dma_start(g_x, x[bass.ds(b, 1), :, :].rearrange("o n d -> n (o d)")
                                 ).then_inc(g_loaded, 16)
                    sp.dma_start(g_adj[:, :], adj[bass.ds(b, 1), :, :].rearrange("o n m -> n (o m)")
                                 ).then_inc(g_loaded, 16)
                    sp.wait_ge(g_out_ready, b + 2)
                    sp.dma_start(out[bass.ds(b, 1), :, :].rearrange("o n d -> n (o d)"), g_out
                                 ).then_inc(g_stored, 16)
                sp.wait_ge(g_stored, 16 * B + 16)

        @block.gpsimd
        def _(pool):
            pool.memset(minus_half[:, :], -0.5).then_inc(half_ready, 1)
            pool.memset(ident[:, :], 0.0).then_inc(const_ready, 1)
            pool.wait_ge(const_ready, 1)
            pool.affine_select(out=ident[:, :], in_=ident[:, :], compare_op=ALU.not_equal, fill=1.0,
                               base=0, pattern=[[-1, 128]], channel_multiplier=1).then_inc(const_ready, 1)
            pool.memset(ones_b[:, :], 1.0).then_inc(const_ready, 1)
            pool.memset(ones[:, :], 1.0).then_inc(const_ready, 1)
            pool.wait_ge(half_ready, 1)

            def coefficients(c, p):
                pool.wait_ge(stats_ready, c + 1)
                if not isinstance(c, int) or c >= 2:
                    pool.wait_ge(normed, c * CHUNK - CHUNK)
                pool.tensor_tensor(rstd[:, p, :], var_eps[:, p, :], minus_half[:, :], ALU.pow
                                   ).then_inc(rstd_ready, 1)
                pool.wait_ge(rstd_ready, c + 1)
                pool.tensor_tensor(shift[:, p, :], mean_neg[:, p, :], rstd[:, p, :], ALU.mult
                                   ).then_inc(coef_ready, 1)

            with_loop = CHUNKS // 2 * 2
            for c in range(2):
                coefficients(c, c)
            with pool.Fori(2, with_loop - 1, 2) as c:
                for j in range(2):
                    coefficients(c + j, j)
            for c in range(with_loop, CHUNKS):
                coefficients(c, c % 2)

            pool.wait_ge(flag_ready, 1)
            with pool.If(pool.value_load(flag[0:1, 0:1], min_val=0, max_val=1) != 0):
                pool.iota(rel_int[:, :], pattern=[[1, NREL]], base=2, channel_multiplier=0
                          ).then_inc(rel_made, 1)
                with pool.Fori(0, B) as b:
                    pool.wait_ge(g_stat_step, b * 3 + 3)
                    pool.tensor_tensor(g_rstd[:, :], g_var[:, :], minus_half[:, 0:1], ALU.pow
                                       ).then_inc(g_rstd_ready, 1)

        @block.scalar
        def _(act):
            act.dma_start(w_raw[:, 0, :], W_loop).then_inc(w_loaded, 16)
            act.dma_start(w_raw[:, 1, :], Wg_loop).then_inc(w_loaded, 16)
            act.dma_start(bias_in[:, 0, :], b_loop.to_broadcast([3, D])).then_inc(bias_loaded, 16)
            act.dma_start(bias_in[:, 1, :], bg_loop.to_broadcast([3, D])).then_inc(bias_loaded, 16)

            def normalise(g, c, phase):
                s, p = phase % 2, phase // CHUNK % 2
                if phase % CHUNK == 0:
                    act.wait_ge(coef_ready, c + 1)
                if late(g):
                    act.wait_ge(turned, g - 1)
                for j in range(GROUP):
                    k = phase % CHUNK * GROUP + j
                    last = nc.scalar.activation(
                        xn[:, s, j * D:j * D + D], x_all[:, bass.ds(g * GC + j * D, D)], ACT.Identity,
                        bias=shift[:, p, k:k + 1], scale=rstd[:, p, k:k + 1])
                last.then_inc(normed, 1)

            def relu_turned(g, phase):
                s = phase % 2
                act.wait_ge(turned, g + 1)
                if late(g):
                    act.wait_ge(val_prod, g - 1)
                nc.scalar.activation(hT[:, s, :], hT_ps[s][:, :], ACT.Relu).then_inc(hT_ready, 1)

            def sigmoid(g, phase):
                s = phase % 2
                act.wait_ge(gate_prod, g + 1)
                if late(g):
                    act.wait_ge(vals_ready, g - 1)
                nc.scalar.activation(gate[:, s, :], gate_ps[s][:, :], ACT.Sigmoid).then_inc(gate_ready, 1)

            def watch(c, phase):
                arrived(act, adj_loaded, c, phase)
                nc.scalar.activation(junk[:, :], adj_all[:, bass.ds(c * CC, CC)], ACT.Relu,
                                     bias=minus_one[:, :],
                                     accum_out=high[:, bass.ds(c, 1)]).then_inc(high_ready, 1)

            def step(t, c, phase):
                if live(t):
                    sigmoid(t, phase)
                if live(t + HT):
                    relu_turned(t + HT, (phase + HT) % UNROLL)
                if live(t + NORM):
                    normalise(t + NORM, chunk_after(c, phase, NORM), (phase + NORM) % UNROLL)
                if phase % 2 == 1 and live(t + 1):
                    watch(chunk_after(c, phase, 1), (phase + 1) % UNROLL)

            act.wait_ge(minus_ready, 1)
            steps(act, step, -NORM, GROUPS)

            act.wait_ge(flag_ready, 1)
            with act.If(act.value_load(flag[0:1, 0:1], min_val=0, max_val=1) != 0):
                with act.Fori(0, B) as b:
                    act.wait_ge(g_turned, b + 1)
                    nc.scalar.activation(g_hT, bank[0][:, 0:D], ACT.Relu)
                    nc.scalar.activation(g_adjT, bank[1][:, 0:N], ACT.Copy).then_inc(g_hT_ready, 1)
                    act.wait_ge(g_prod, b + 1)
                    nc.scalar.activation(g_P, bank[2][:, 0:3 * D], ACT.Copy)
                    nc.scalar.activation(g_G, bank[3][:, 0:3 * D], ACT.Copy).then_inc(g_PG, 1)
                    act.wait_ge(l_in_ready, b + 1)
                    nc.scalar.activation(g_gate[2], g_gatein[2], ACT.Sigmoid).then_inc(l_gate_ready, 1)
                    with act.Fori(0, BLOCKS) as k:
                        for d in range(2):
                            act.wait_ge(g_in_ready, b * UNITS + k * 2 + (d + 1))
                            nc.scalar.activation(g_gate[d], g_gatein[d], ACT.Sigmoid
                                                 ).then_inc(g_gate_ready, 1)

        @block.vector
        def _(dve):
            nc.vector.memset(minus_one[:, :], -1.0).then_inc(minus_ready, 1)
            nc.vector.memset(bias_rows[:, :, :], 0.0).then_inc(bias_step, 1)

            def row_stats(g, c, phase):
                p = phase // CHUNK % 2
                if phase % CHUNK == 0:
                    arrived(dve, x_loaded, c, phase)
                for j in range(GROUP):
                    k = phase % CHUNK * GROUP + j
                    last = nc.vector.bn_stats(stats[:, p, k, :], x_all[:, bass.ds(g * GC + j * D, D)])
                if phase % CHUNK == CHUNK - 1:
                    last.then_inc(stat_step, 1)
                    st = stats[:, p, :, :]
                    dve.wait_ge(stat_step, c * 3 + 1)
                    nc.vector.scalar_tensor_tensor(out=sum_neg[:, :], in0=st[:, :, 1], scalar=-1.0,
                                                   in1=st[:, :, 4], op0=ALU.mult, op1=ALU.subtract)
                    nc.vector.tensor_tensor(squares[:, :], st[:, :, 2], st[:, :, 5], ALU.add)
                    nc.vector.tensor_tensor(diff[:, :], st[:, :, 1], st[:, :, 4], ALU.subtract
                                            ).then_inc(stat_step, 1)
                    dve.wait_ge(stat_step, c * 3 + 2)
                    nc.vector.tensor_tensor(diff_sq[:, :], diff[:, :], diff[:, :], ALU.mult
                                            ).then_inc(stat_step, 1)
                    if late(g, 2 * CHUNK):
                        dve.wait_ge(coef_ready, c - 1)
                    nc.vector.tensor_scalar(mean_neg[:, p, :], sum_neg[:, :], 0.5, None, ALU.mult)
                    dve.wait_ge(stat_step, c * 3 + 3)
                    nc.vector.scalar_tensor_tensor(out=var4[:, :], in0=squares[:, :], scalar=4.0 / D,
                                                   in1=diff_sq[:, :], op0=ALU.mult, op1=ALU.add
                                                   ).then_inc(var_step, 1)
                    dve.wait_ge(var_step, c + 1)
                    nc.vector.tensor_scalar(var_eps[:, p, :], var4[:, :], 0.25, EPS, ALU.mult, ALU.add
                                            ).then_inc(stats_ready, 1)

            def messages(g, phase):
                s = phase % 2
                dve.wait_ge(val_prod, g + 1)
                dve.wait_ge(gate_ready, g + 1)
                if late(g):
                    dve.wait_ge(summed, g - 1)
                nc.vector.tensor_tensor(vals[:, s, :], val_ps[s][:, :], gate[:, s, :], ALU.mult
                                        ).then_inc(vals_ready, 1)

            def edges(g, c, phase):
                s = phase % 2
                if phase % CHUNK == 0:
                    arrived(dve, adj_loaded, c, phase)
                if late(g):
                    dve.wait_ge(summed, g - 1)
                nc.vector.tensor_scalar(mask[:, s, :], adj_all[:, bass.ds(g * GC, GC)], 1.0, None,
                                        ALU.is_equal).then_inc(mask_ready, 1)

            def output(g, phase):
                s = phase % 2
                dve.wait_ge(summed, g + 1)
                cols = x_all[:, bass.ds(g * GC, GC)]
                nc.vector.scalar_tensor_tensor(out=cols, in0=agg_ps[s][:, :], scalar=0.0, in1=cols,
                                               op0=ALU.max, op1=ALU.add).then_inc(out_ready, 1)

            def step(t, c, phase):
                if live(t):
                    messages(t, phase)
                if live(t - 1):
                    output(t - 1, (phase - 1) % UNROLL)
                if live(t + 1):
                    edges(t + 1, chunk_after(c, phase, 1), (phase + 1) % UNROLL)
                if live(t + STATS):
                    row_stats(t + STATS, chunk_after(c, phase, STATS), (phase + STATS) % UNROLL)

            dve.wait_ge(w_turned, 1)
            nc.vector.tensor_copy(w_loop[:, 0, :], bank[6][:, 0:128])
            nc.vector.tensor_copy(w_gT[:, :], bank[6][:, 128:256]).then_inc(w_copied, 1)
            dve.wait_ge(w_turned, 2)
            nc.vector.tensor_copy(w_loop[:, 1, :], bank[7][:, 0:128]).then_inc(w_copied, 1)

            dve.wait_ge(bias_loaded, 32)
            b_row = bias_in[:, :, :].rearrange("p a d -> p (a d)")
            nc.vector.tensor_copy(part[0][:, :], b_row).then_inc(bias_step, 1)
            dve.wait_ge(bias_step, 2)
            nc.vector.tensor_tensor(rest[0][:, :], b_row, part[0][:, :], ALU.subtract).then_inc(bias_step, 1)
            dve.wait_ge(bias_step, 3)
            nc.vector.tensor_copy(part[1][:, :], rest[0][:, :]).then_inc(bias_step, 1)
            dve.wait_ge(bias_step, 4)
            nc.vector.tensor_tensor(rest[1][:, :], rest[0][:, :], part[1][:, :], ALU.subtract
                                    ).then_inc(bias_step, 1)
            dve.wait_ge(bias_step, 5)
            nc.vector.tensor_copy(part[2][:, :], rest[1][:, :]).then_inc(bias_step, 1)
            dve.wait_ge(const_ready, 4)
            nc.vector.tensor_scalar(mix[0][:, :], part[0][:, :], ident[0:3, 0:1], None, ALU.mult
                                    ).then_inc(bias_step, 1)
            dve.wait_ge(bias_step, 7)
            nc.vector.scalar_tensor_tensor(out=mix[1][:, :], in0=part[1][:, :], scalar=ident[0:3, 1:2],
                                           in1=mix[0][:, :], op0=ALU.mult, op1=ALU.add).then_inc(bias_step, 1)
            dve.wait_ge(bias_step, 8)
            nc.vector.scalar_tensor_tensor(out=mix[0][:, :], in0=part[2][:, :], scalar=ident[0:3, 2:3],
                                           in1=mix[1][:, :], op0=ALU.mult, op1=ALU.add).then_inc(bias_step, 1)
            dve.wait_ge(bias_step, 9)
            for a in range(2):
                for j in range(GROUP):
                    nc.vector.tensor_copy(bias_rows[0:3, a, j * D:j * D + D], mix[0][:, a * D:a * D + D]
                                          ).then_inc(bias_step, 1)

            steps(dve, step, -STATS, GROUPS + 1)

            dve.wait_ge(high_total, 1)
            nc.vector.reduce_sum(high_sum[:, :], bank[0][0:1, 0:CHUNKS], axis=AX.X).then_inc(flag_step, 1)
            dve.wait_ge(flag_step, 1)
            nc.vector.tensor_scalar(flag[:, :], high_sum[:, :], 0.5, None, ALU.is_gt).then_inc(flag_ready, 1)

            dve.wait_ge(flag_ready, 1)
            with dve.If(dve.value_load(flag[0:1, 0:1], min_val=0, max_val=1) != 0):
                dve.wait_ge(rel_made, 1)
                nc.vector.tensor_copy(rel_id[:, :], rel_int[:, :]).then_inc(g_summed, 1)
                nc.vector.tensor_copy(g_W[:, 2 * D:3 * D], w_loop[:, 0, :]).then_inc(g_summed, 1)
                nc.vector.tensor_copy(g_C[:, 2 * D:3 * D], w_loop[:, 1, :]).then_inc(g_out_ready, 1)
                for d in range(2):
                    dve.wait_ge(g_w_turned, 2 * d + 1)
                    nc.vector.tensor_copy(g_W[:, d * D:d * D + D], bank[6][:, 0:128])
                    nc.vector.tensor_copy(g_wgT[:, d * D:d * D + D], bank[6][:, 128:256]
                                          ).then_inc(g_setup, 1)
                    dve.wait_ge(g_w_turned, 2 * d + 2)
                    nc.vector.tensor_copy(g_C[:, d * D:d * D + D], bank[7][:, 0:128]).then_inc(g_setup, 1)
                dve.wait_ge(tab_loaded, 16 * 10)

                def wide(ap, n):
                    return ap.unsqueeze(1).to_broadcast([128, n, D])

                def blocks(ap, n):
                    return ap.rearrange("p (r d) -> p r d", r=n)

                with dve.Fori(0, B) as b:
                    dve.wait_ge(g_loaded, b * 32 + 32)
                    nc.vector.bn_stats(g_stats[:, :], g_x).then_inc(g_stat_step, 1)
                    dve.wait_ge(g_stat_step, b * 3 + 1)
                    nc.vector.tensor_copy(g_adjf, g_adj[:, :])
                    nc.vector.bn_aggr(g_moments[:, :], g_stats[:, :]).then_inc(g_stat_step, 1)
                    dve.wait_ge(g_stat_step, b * 3 + 2)
                    nc.vector.tensor_scalar(g_var[:, :], g_moments[:, 1:2], EPS, None, ALU.add
                                            ).then_inc(g_stat_step, 1)
                    dve.wait_ge(g_rstd_ready, b + 1)
                    nc.vector.tensor_scalar(g_xn, g_x, g_moments[:, 0:1], g_rstd[:, 0:1],
                                            ALU.subtract, ALU.mult).then_inc(g_normed, 1)

                    dve.wait_ge(g_PG, b + 1)
                    nc.vector.tensor_tensor(g_gatein[2], g_G[:, 2 * D:3 * D], bg_loop_tab, ALU.add
                                            ).then_inc(l_in_ready, 1)
                    nc.vector.tensor_scalar(g_mask[2], g_adjf, 1.0, None, ALU.is_equal)
                    nc.vector.tensor_tensor(g_vals[2], g_P[:, 2 * D:3 * D], b_loop_tab, ALU.add
                                            ).then_inc(l_val_step, 1)
                    dve.wait_ge(l_val_step, b + 1)
                    dve.wait_ge(l_gate_ready, b + 1)
                    nc.vector.tensor_tensor(g_vals[2], g_vals[2], g_gate[2], ALU.mult
                                            ).then_inc(l_vals_ready, 1)

                    with dve.Fori(0, BLOCKS) as k:
                        for d in range(2):
                            nc.vector.tensor_tensor(
                                blocks(g_gatein[d], REL_BLOCK), wide(g_G[:, d * D:d * D + D], REL_BLOCK),
                                blocks(bg_tab[d][:, bass.ds(k * RB, RB)], REL_BLOCK), ALU.add
                            ).then_inc(g_in_ready, 1)
                        for d in range(2):
                            dve.wait_ge(g_summed, b * UNITS + k * 2 + (d + 1))
                            nc.vector.tensor_tensor(
                                blocks(g_mask[d], REL_BLOCK), wide((g_adjT, g_adjf)[d], REL_BLOCK),
                                rel_id[:, bass.ds(k * REL_BLOCK, REL_BLOCK)].unsqueeze(2)
                                .to_broadcast([128, REL_BLOCK, N]), ALU.is_equal)
                            nc.vector.tensor_tensor(
                                blocks(g_vals[d], REL_BLOCK), wide(g_P[:, d * D:d * D + D], REL_BLOCK),
                                blocks(b_tab[d][:, bass.ds(k * RB, RB)], REL_BLOCK), ALU.add
                            ).then_inc(g_val_step, 1)
                            dve.wait_ge(g_val_step, b * UNITS + k * 2 + (d + 1))
                            dve.wait_ge(g_gate_ready, b * UNITS + k * 2 + (d + 1))
                            nc.vector.tensor_tensor(g_vals[d], g_vals[d], g_gate[d], ALU.mult
                                                    ).then_inc(g_vals_ready, 1)

                    dve.wait_ge(g_summed, b * UNITS + (UNITS + 2))
                    nc.vector.scalar_tensor_tensor(out=g_out, in0=bank[4][:, 0:D], scalar=0.0, in1=g_x,
                                                   op0=ALU.max, op1=ALU.add).then_inc(g_out_ready, 1)

        @block.tensor
        def _(pe):
            def turn_weights(raw_w, raw_g, gT, ready, copied, at):
                nc.tensor.transpose(bank[6][:, 0:128], raw_w, ident[:, :])
                nc.tensor.transpose(bank[6][:, 128:256], raw_g, ident[:, :]).then_inc(ready, 1)
                pe.wait_ge(copied, at)
                nc.tensor.matmul(bank[7][:, 0:128], raw_w, gT, start=True, stop=True).then_inc(ready, 1)

            pe.wait_ge(const_ready, 4)
            pe.wait_ge(w_loaded, 32)
            turn_weights(w_raw[:, 0, :], w_raw[:, 1, :], w_gT[:, :], w_turned, w_copied, 1)

            def turn_rows(g, phase):
                s = phase % 2
                pe.wait_ge(normed, g + 1)
                if late(g):
                    pe.wait_ge(hT_ready, g - 1)
                for j in range(GROUP):
                    last = nc.tensor.transpose(hT_ps[s][:, j * N:j * N + N], xn[:, s, j * D:j * D + D],
                                               ident[:, :])
                last.then_inc(turned, 1)

            def products(g, phase):
                s = phase % 2
                pe.wait_ge(hT_ready, g + 1)
                for a, ps, free, ready in ((1, gate_ps[s], gate_ready, gate_prod),
                                           (0, val_ps[s], vals_ready, val_prod)):
                    if late(g):
                        pe.wait_ge(free, g - 1)
                    nc.tensor.matmul(ps[:, :], ones_b[:, :], bias_rows[:, a, :], start=True, stop=False)
                    for j in range(GROUP):
                        last = nc.tensor.matmul(ps[:, j * D:j * D + D], hT[:, s, j * N:j * N + N],
                                                w_loop[:, a, :], start=False, stop=(j == GROUP - 1))
                    last.then_inc(ready, 1)

            def aggregate(g, phase):
                s = phase % 2
                pe.wait_ge(mask_ready, g + 1)
                pe.wait_ge(vals_ready, g + 1)
                if late(g):
                    pe.wait_ge(out_ready, g - 1)
                for j in range(GROUP):
                    last = nc.tensor.matmul(agg_ps[s][:, j * D:j * D + D], mask[:, s, j * N:j * N + N],
                                            vals[:, s, j * D:j * D + D], start=True, stop=True)
                last.then_inc(summed, 1)

            def step(t, c, phase):
                if live(t + HT):
                    turn_rows(t + HT, (phase + HT) % UNROLL)
                if live(t + PROD):
                    if isinstance(t, int) and t == -PROD:
                        pe.wait_ge(w_copied, 2)
                        pe.wait_ge(bias_step, 9 + 2 * GROUP)
                    products(t + PROD, (phase + PROD) % UNROLL)
                if live(t):
                    aggregate(t, phase)

            steps(pe, step, -HT, GROUPS)

            pe.wait_ge(high_ready, CHUNKS)
            pe.wait_ge(hT_ready, GROUPS)
            nc.tensor.matmul(bank[0][0:1, 0:CHUNKS], ones[:, :], high[:, :], start=True, stop=True
                             ).then_inc(high_total, 1)

            pe.wait_ge(flag_ready, 1)
            with pe.If(pe.value_load(flag[0:1, 0:1], min_val=0, max_val=1) != 0):
                pe.wait_ge(tab_loaded, 16 * 10)
                for d in range(2):
                    if d:
                        pe.wait_ge(g_setup, 2)
                    turn_weights(g_wraw[:, 2 * d * D:2 * d * D + D],
                                 g_wraw[:, 2 * d * D + D:2 * d * D + 2 * D],
                                 g_wgT[:, d * D:d * D + D], g_w_turned, g_setup, 2 * d + 1)
                pe.wait_ge(g_setup, 4)
                with pe.Fori(0, B) as b:
                    pe.wait_ge(g_normed, b + 1)
                    nc.tensor.transpose(bank[0][:, 0:N], g_xn, ident[:, :])
                    nc.tensor.transpose(bank[1][:, 0:N], g_adjf, ident[:, :]).then_inc(g_turned, 1)
                    pe.wait_ge(g_hT_ready, b + 1)
                    nc.tensor.matmul(bank[2][:, 0:3 * D], g_hT, g_W, start=True, stop=True)
                    nc.tensor.matmul(bank[3][:, 0:3 * D], g_hT, g_C, start=True, stop=True
                                     ).then_inc(g_prod, 1)
                    pe.wait_ge(l_vals_ready, b + 1)
                    pe.wait_ge(g_out_ready, b + 1)
                    nc.tensor.matmul(bank[4][:, 0:D], g_mask[2], g_vals[2], start=True, stop=False,
                                     skip_group_check=True)
                    with pe.Fori(0, BLOCKS) as k:
                        for d in range(2):
                            pe.wait_ge(g_vals_ready, b * UNITS + k * 2 + (d + 1))
                            for r in range(REL_BLOCK):
                                last = nc.tensor.matmul(bank[4][:, 0:D], g_mask[d][:, r * N:r * N + N],
                                                        g_vals[d][:, r * D:r * D + D], start=False,
                                                        stop=False, skip_group_check=True)
                            last.then_inc(g_summed, 1)


_INS = ["x", "adj", "L0_gnn_W_fwd", "L0_gnn_W_bwd", "L0_gnn_W_loop", "L0_gnn_Wg_fwd", "L0_gnn_Wg_bwd",
        "L0_gnn_Wg_loop", "L0_gnn_b_fwd", "L0_gnn_b_bwd", "L0_gnn_b_loop", "L0_gnn_bg_fwd",
        "L0_gnn_bg_bwd", "L0_gnn_bg_loop"]


def kernel(**inputs):
    import concourse.bacc as bacc
    from concourse.bass_utils import run_bass_kernel_spmd

    nc = bacc.Bacc("TRN2", target_bir_lowering=False, num_devices=1)
    arrays, args = {}, []
    for name in _INS:
        a = np.ascontiguousarray(inputs[name])
        arrays[f"in_{name}"] = a
        args.append(nc.dram_tensor(f"in_{name}", a.shape, mybir.dt.from_np(a.dtype), kind="ExternalInput").ap())
    out = nc.dram_tensor("out", arrays["in_x"].shape, FP32, kind="ExternalOutput").ap()
    build(nc, *args, out)
    r = run_bass_kernel_spmd(nc, [arrays], core_ids=[0])
    return r.results[0]["out"]
```

```python
from contextlib import ExitStack

import numpy as np
import concourse.bass as bass
from concourse import mybir

FP32, FP32R, BF16, INT32 = mybir.dt.float32, mybir.dt.float32r, mybir.dt.bfloat16, mybir.dt.int32
ALU = mybir.AluOpType
ACT = mybir.ActivationFunctionType
AX = mybir.AxisListType

EPS = 1e-5
GROUP = 4
CHUNK = 2
UNROLL = 4
REL_BLOCK = 3


def build(nc, x, adj, W_fwd, W_bwd, W_loop, Wg_fwd, Wg_bwd, Wg_loop,
          b_fwd, b_bwd, b_loop, bg_fwd, bg_bwd, bg_loop, out):
    B, N, D = x.shape
    NREL = b_fwd.shape[0]
    assert N == 128 and D == 128 and B % (GROUP * CHUNK) == 0 and NREL % REL_BLOCK == 0
    GROUPS = B // GROUP
    CHUNKS = GROUPS // CHUNK
    GC = GROUP * D
    CG = GROUP * CHUNK
    CC = CG * D

    STATS, COEF, NORM, HT, PROD = 6, 4, 3, 2, 1
    LOOP_FROM = 2
    LOOP_TO = LOOP_FROM + (GROUPS - STATS - LOOP_FROM) // UNROLL * UNROLL
    assert LOOP_TO > LOOP_FROM
    LOAD_AHEAD = 6

    ctx = ExitStack()
    with ctx:
        def sb(name, shape, dt=FP32):
            return ctx.enter_context(nc.sbuf_tensor(name, shape, dt))

        def sem(name):
            return ctx.enter_context(nc.semaphore(name))

        SIDE = max(B * D, 2 * NREL * D + 36 * D)
        x_all = sb("x_all", [128, SIDE])
        adj_all = sb("adj_all", [128, SIDE], INT32)
        xn = sb("xn", [128, 2, GC])
        hT_hi = sb("hT_hi", [128, 2, GC], FP32R)
        hT_lo = sb("hT_lo", [128, 2, GC], FP32R)
        gate = sb("gate", [128, 2, GC])
        vals = sb("vals", [128, 2, GC])
        mask = sb("mask", [128, 2, GROUP * N])
        stats = sb("stats", [128, 2, CG, 6])
        sum_neg = sb("sum_neg", [128, CG])
        diff = sb("diff", [128, CG])
        diff_sq = sb("diff_sq", [128, CG])
        squares = sb("squares", [128, CG])
        var4 = sb("var4", [128, CG])
        mean_neg = sb("mean_neg", [128, 2, CG])
        var_eps = sb("var_eps", [128, 2, CG])
        rstd = sb("rstd", [128, 2, CG])
        shift = sb("shift", [128, 2, CG])
        minus_half = sb("minus_half", [128, CG])
        minus_half_1 = minus_half[:, 0:1]
        ident = sb("ident", [128, 128])
        ones = sb("ones", [128, 1])
        w_raw = sb("w_raw", [128, 2, 128])
        w_gT = sb("w_gT", [128, 128])
        w_hi = sb("w_hi", [128, 2 * D], FP32R)
        w_lo = sb("w_lo", [128, 2 * D], FP32R)
        w_loop = sb("w_loop", [128, 2, D])
        ones_b = sb("ones_b", [128, 128], BF16)
        bias_rows = sb("bias_rows", [128, 2, 2 * D], BF16)
        bias_in = sb("bias_in", [3, 2, D])
        part = [sb(f"part{n}", [3, 2 * D], BF16) for n in range(3)]
        rest = [sb(f"rest{n}", [3, 2 * D]) for n in range(2)]
        mix = [sb(f"mix{n}", [3, 2 * D]) for n in range(2)]
        junk = sb("junk", [128, CC], BF16)
        dist = sb("dist", [128, CHUNKS])
        dist_sum = sb("dist_sum", [1, 1])
        flag = sb("flag", [1, 1], INT32)

        psum = ctx.enter_context(nc.psum_tensor("psum", [128, 8 * 512], FP32))
        bank = [psum[:, n * 512:n * 512 + 512] for n in range(8)]
        hT_ps, agg_ps = bank[0:2], bank[6:8]
        prod_ps = [psum[:, n * 1024:n * 1024 + 1024].rearrange("p (g a d) -> p g a d", g=GROUP, a=2)
                   for n in (1, 2)]

        x_loaded = [sem(f"x_loaded{n}") for n in range(2)]
        adj_loaded = [sem(f"adj_loaded{n}") for n in range(2)]
        w_loaded = sem("w_loaded")
        bias_loaded = sem("bias_loaded")
        const_ready = sem("const_ready")
        half_ready = sem("half_ready")
        w_turned = sem("w_turned")
        w_copied = sem("w_copied")
        bias_step = sem("bias_step")
        stat_step = sem("stat_step")
        var_step = sem("var_step")
        stats_ready = sem("stats_ready")
        rstd_ready = sem("rstd_ready")
        coef_ready = sem("coef_ready")
        normed = sem("normed")
        turned = sem("turned")
        hi_ready = sem("hi_ready")
        hT_ready = sem("hT_ready")
        prod_ready = sem("prod_ready")
        w_split = sem("w_split")
        gate_ready = sem("gate_ready")
        vals_ready = sem("vals_ready")
        mask_ready = sem("mask_ready")
        summed = sem("summed")
        out_ready = sem("out_ready")
        stored = sem("stored")
        dist_ready = sem("dist_ready")
        dist_total = sem("dist_total")
        flag_step = sem("flag_step")
        flag_ready = sem("flag_ready")

        adj_f32 = adj_all[:, :].bitcast(FP32)
        TABLE = NREL * D
        room = {"x": 0, "a": 0}

        def view(side, cols):
            base = x_all[:, :] if side == "x" else adj_f32
            at = room[side]
            room[side] += cols
            assert room[side] <= SIDE
            return base[:, at:at + cols]

        DIRS = (("fwd", W_fwd, Wg_fwd), ("bwd", W_bwd, Wg_bwd))
        b_tab = [view("x", TABLE) for _ in DIRS]
        bg_tab = [view("a", TABLE) for _ in DIRS]
        RB = REL_BLOCK * D
        g_x, g_xn, g_hT, g_adjf, g_adjT, g_out = (view("x", D) for _ in range(6))
        g_vals = [view("x", RB) for _ in range(2)] + [view("x", D)]
        g_P = view("x", 3 * D)
        b_loop_tab = view("x", D)
        g_W = view("x", 3 * D)
        g_gatein = [view("a", RB) for _ in range(2)] + [view("a", D)]
        g_gate = [view("a", RB) for _ in range(2)] + [view("a", D)]
        g_mask = [view("a", RB) for _ in range(2)] + [view("a", D)]
        g_G = view("a", 3 * D)
        bg_loop_tab = view("a", D)
        g_C = view("a", 3 * D)
        g_wraw = view("a", 4 * D)
        g_wgT = view("a", 2 * D)
        g_adj = sb("g_adj", [128, N], INT32)
        g_stats = sb("g_stats", [128, 6])
        g_moments = sb("g_moments", [128, 2])
        g_var = sb("g_var", [128, 1])
        g_rstd = sb("g_rstd", [128, 1])
        rel_int = sb("rel_int", [128, NREL], INT32)
        rel_id = sb("rel_id", [128, NREL])
        BLOCKS = NREL // REL_BLOCK
        UNITS = 2 * BLOCKS

        tab_loaded = sem("tab_loaded")
        rel_made = sem("rel_made")
        g_setup = sem("g_setup")
        g_w_turned = sem("g_w_turned")
        g_loaded = sem("g_loaded")
        g_stat_step = sem("g_stat_step")
        g_rstd_ready = sem("g_rstd_ready")
        g_normed = sem("g_normed")
        g_turned = sem("g_turned")
        g_hT_ready = sem("g_hT_ready")
        g_prod = sem("g_prod")
        g_PG = sem("g_PG")
        g_in_ready = sem("g_in_ready")
        g_gate_ready = sem("g_gate_ready")
        g_val_step = sem("g_val_step")
        g_vals_ready = sem("g_vals_ready")
        g_summed = sem("g_summed")
        l_in_ready = sem("l_in_ready")
        l_gate_ready = sem("l_gate_ready")
        l_val_step = sem("l_val_step")
        l_vals_ready = sem("l_vals_ready")
        g_out_ready = sem("g_out_ready")
        g_stored = sem("g_stored")

        def per_graph(ap):
            return ap.rearrange("p (g d) -> p g d", g=GROUP)

        def live(g):
            return not isinstance(g, int) or 0 <= g < GROUPS

        def late(g, slots=2):
            return not isinstance(g, int) or g >= slots

        def steps(eng, step, first, last):
            for t in range(first, LOOP_FROM):
                step(t, t // CHUNK, t % UNROLL)
            with eng.Fori(LOOP_FROM // CHUNK, (LOOP_TO - UNROLL) // CHUNK + 1, UNROLL // CHUNK) as c:
                for j in range(UNROLL):
                    step(c * CHUNK + j, c + j // CHUNK, (LOOP_FROM + j) % UNROLL)
            for t in range(LOOP_TO, last):
                step(t, t // CHUNK, t % UNROLL)

        def chunk_after(c, phase, ahead):
            return c + (phase % CHUNK + ahead) // CHUNK

        def arrived(eng, loaded, c, phase):
            p = phase // CHUNK % 2
            eng.wait_ge(loaded[p], (c - p) * 8 + 16)

        block = ctx.enter_context(nc.Block())

        @block.sync
        def _(sp):
            def places(c):
                if isinstance(c, int):
                    return c * CG, c * CC
                return sp.snap(c * CG), sp.snap(c * CC)

            def load(c, p):
                at, col = places(c)
                if not isinstance(c, int) or c >= 2:
                    sp.wait_ge(x_loaded[p], (c - p) * 8)
                    sp.wait_ge(adj_loaded[p], (c - p) * 8)
                sp.dma_start(x_all[:, bass.ds(col, CC)].rearrange("p (b d) -> p b d", b=CG),
                             x[bass.ds(at, CG), :, :].rearrange("b n d -> n b d")).then_inc(x_loaded[p], 16)
                sp.dma_start(adj_all[:, bass.ds(col, CC)].rearrange("p (b n) -> p b n", b=CG),
                             adj[bass.ds(at, CG), :, :].rearrange("b n m -> n b m")
                             ).then_inc(adj_loaded[p], 16)

            def store(c):
                at, col = places(c)
                sp.wait_ge(out_ready, c * CHUNK + CHUNK)
                sp.dma_start(out[bass.ds(at, CG), :, :].rearrange("b n d -> n b d"),
                             x_all[:, bass.ds(col, CC)].rearrange("p (b d) -> p b d", b=CG)
                             ).then_inc(stored, 16)

            ahead = min(LOAD_AHEAD, CHUNKS)
            for c in range(ahead):
                load(c, c % 2)
            even = (CHUNKS - ahead) // 2 * 2
            if even:
                with sp.Fori(ahead, ahead + even - 1, 2) as c:
                    for j in range(2):
                        load(c + j, (ahead + j) % 2)
                        store(c + j - ahead)
            for c in range(even, CHUNKS):
                store(c)
            sp.wait_ge(stored, 16 * CHUNKS)

            sp.wait_ge(flag_ready, 1)
            with sp.If(sp.value_load(flag[0:1, 0:1], min_val=0, max_val=1) != 0):
                for d, (b_, bg_) in enumerate(((b_fwd, bg_fwd), (b_bwd, bg_bwd))):
                    sp.dma_start(b_tab[d], b_.rearrange("(o r) d -> o (r d)", o=1).to_broadcast([128, TABLE])
                                 ).then_inc(tab_loaded, 16)
                    sp.dma_start(bg_tab[d], bg_.rearrange("(o r) d -> o (r d)", o=1).to_broadcast([128, TABLE])
                                 ).then_inc(tab_loaded, 16)
                sp.dma_start(b_loop_tab, b_loop.to_broadcast([128, D])).then_inc(tab_loaded, 16)
                sp.dma_start(bg_loop_tab, bg_loop.to_broadcast([128, D])).then_inc(tab_loaded, 16)
                for d, (_, W, Wg) in enumerate(DIRS):
                    sp.dma_start(g_wraw[:, 2 * d * D:2 * d * D + D], W).then_inc(tab_loaded, 16)
                    sp.dma_start(g_wraw[:, 2 * d * D + D:2 * d * D + 2 * D], Wg).then_inc(tab_loaded, 16)
                sp.sem_inc(g_stored, 16)
                with sp.Fori(0, B) as b:
                    sp.wait_ge(g_stored, b * 16 + 16)
                    sp.dma_start(g_x, x[bass.ds(b, 1), :, :].rearrange("o n d -> n (o d)")
                                 ).then_inc(g_loaded, 16)
                    sp.dma_start(g_adj[:, :], adj[bass.ds(b, 1), :, :].rearrange("o n m -> n (o m)")
                                 ).then_inc(g_loaded, 16)
                    sp.wait_ge(g_out_ready, b + 2)
                    sp.dma_start(out[bass.ds(b, 1), :, :].rearrange("o n d -> n (o d)"), g_out
                                 ).then_inc(g_stored, 16)
                sp.wait_ge(g_stored, 16 * B + 16)

        @block.gpsimd
        def _(pool):
            pool.memset(minus_half[:, :], -0.5).then_inc(half_ready, 1)
            pool.memset(ident[:, :], 0.0).then_inc(const_ready, 1)
            pool.wait_ge(const_ready, 1)
            pool.affine_select(out=ident[:, :], in_=ident[:, :], compare_op=ALU.not_equal, fill=1.0,
                               base=0, pattern=[[-1, 128]], channel_multiplier=1).then_inc(const_ready, 1)
            pool.memset(ones_b[:, :], 1.0).then_inc(const_ready, 1)
            pool.memset(ones[:, :], 1.0).then_inc(const_ready, 1)
            pool.wait_ge(half_ready, 1)

            def coefficients(c, p):
                pool.wait_ge(stats_ready, c + 1)
                if not isinstance(c, int) or c >= 2:
                    pool.wait_ge(normed, c * CHUNK - CHUNK)
                pool.tensor_tensor(rstd[:, p, :], var_eps[:, p, :], minus_half[:, :], ALU.pow
                                   ).then_inc(rstd_ready, 1)
                pool.wait_ge(rstd_ready, c + 1)
                pool.tensor_tensor(shift[:, p, :], mean_neg[:, p, :], rstd[:, p, :], ALU.mult
                                   ).then_inc(coef_ready, 1)

            def edges(g, c, phase):
                s = phase % 2
                if phase % CHUNK == 0:
                    arrived(pool, adj_loaded, c, phase)
                if late(g):
                    pool.wait_ge(summed, g - 1)
                pool.tensor_copy(mask[:, s, :], adj_all[:, bass.ds(g * GC, GC)]).then_inc(mask_ready, 1)

            def step(t, c, phase):
                if phase % CHUNK == 0 and live(t + COEF):
                    coefficients(chunk_after(c, phase, COEF), (phase + COEF) // CHUNK % 2)
                if live(t + 1):
                    edges(t + 1, chunk_after(c, phase, 1), (phase + 1) % UNROLL)

            steps(pool, step, -COEF, GROUPS)

            pool.wait_ge(flag_ready, 1)
            with pool.If(pool.value_load(flag[0:1, 0:1], min_val=0, max_val=1) != 0):
                pool.iota(rel_int[:, :], pattern=[[1, NREL]], base=2, channel_multiplier=0
                          ).then_inc(rel_made, 1)
                with pool.Fori(0, B) as b:
                    pool.wait_ge(g_stat_step, b * 3 + 3)
                    pool.tensor_tensor(g_rstd[:, :], g_var[:, :], minus_half[:, 0:1], ALU.pow
                                       ).then_inc(g_rstd_ready, 1)

        @block.scalar
        def _(act):
            act.preload_act_table(ACT.Sigmoid)
            act.dma_start(w_raw[:, 0, :], W_loop).then_inc(w_loaded, 16)
            act.dma_start(w_raw[:, 1, :], Wg_loop).then_inc(w_loaded, 16)
            act.dma_start(bias_in[:, 0, :], b_loop.to_broadcast([3, D])).then_inc(bias_loaded, 16)
            act.dma_start(bias_in[:, 1, :], bg_loop.to_broadcast([3, D])).then_inc(bias_loaded, 16)

            def normalise(g, c, phase):
                s, p = phase % 2, phase // CHUNK % 2
                if phase % CHUNK == 0:
                    act.wait_ge(coef_ready, c + 1)
                if late(g):
                    act.wait_ge(turned, g - 1)
                for j in range(GROUP):
                    k = phase % CHUNK * GROUP + j
                    last = nc.scalar.activation(
                        xn[:, s, j * D:j * D + D], x_all[:, bass.ds(g * GC + j * D, D)], ACT.Identity,
                        bias=shift[:, p, k:k + 1], scale=rstd[:, p, k:k + 1])
                last.then_inc(normed, 1)

            def relu_turned(g, phase):
                s = phase % 2
                act.wait_ge(turned, g + 1)
                if late(g):
                    act.wait_ge(prod_ready, g - 1)
                nc.scalar.activation(hT_hi[:, s, :], hT_ps[s], ACT.Relu).then_inc(hi_ready, 1)

            def sigmoid(g, phase):
                s = phase % 2
                act.wait_ge(prod_ready, g + 1)
                if late(g):
                    act.wait_ge(vals_ready, g - 1)
                nc.scalar.activation(per_graph(gate[:, s, :]), prod_ps[s][:, :, 1, :], ACT.Sigmoid
                                     ).then_inc(gate_ready, 1)

            def watch(c, phase):
                arrived(act, adj_loaded, c, phase)
                nc.scalar.activation(junk[:, :], adj_all[:, bass.ds(c * CC, CC)], ACT.Abs,
                                     bias=minus_half_1,
                                     accum_out=dist[:, bass.ds(c, 1)]).then_inc(dist_ready, 1)

            def step(t, c, phase):
                if live(t):
                    sigmoid(t, phase)
                if live(t + HT):
                    relu_turned(t + HT, (phase + HT) % UNROLL)
                if live(t + NORM):
                    normalise(t + NORM, chunk_after(c, phase, NORM), (phase + NORM) % UNROLL)
                if phase % 2 == 1 and live(t + 1):
                    watch(chunk_after(c, phase, 1), (phase + 1) % UNROLL)

            act.wait_ge(half_ready, 1)
            steps(act, step, -NORM, GROUPS)

            act.wait_ge(flag_ready, 1)
            with act.If(act.value_load(flag[0:1, 0:1], min_val=0, max_val=1) != 0):
                with act.Fori(0, B) as b:
                    act.wait_ge(g_turned, b + 1)
                    nc.scalar.activation(g_hT, bank[0][:, 0:D], ACT.Relu)
                    nc.scalar.activation(g_adjT, bank[1][:, 0:N], ACT.Copy).then_inc(g_hT_ready, 1)
                    act.wait_ge(g_prod, b + 1)
                    nc.scalar.activation(g_P, bank[2][:, 0:3 * D], ACT.Copy)
                    nc.scalar.activation(g_G, bank[3][:, 0:3 * D], ACT.Copy).then_inc(g_PG, 1)
                    act.wait_ge(l_in_ready, b + 1)
                    nc.scalar.activation(g_gate[2], g_gatein[2], ACT.Sigmoid).then_inc(l_gate_ready, 1)
                    with act.Fori(0, BLOCKS) as k:
                        for d in range(2):
                            act.wait_ge(g_in_ready, b * UNITS + k * 2 + (d + 1))
                            nc.scalar.activation(g_gate[d], g_gatein[d], ACT.Sigmoid
                                                 ).then_inc(g_gate_ready, 1)

        @block.vector
        def _(dve):
            nc.vector.memset(bias_rows[:, :, :], 0.0).then_inc(bias_step, 1)

            def row_stats(g, c, phase):
                p = phase // CHUNK % 2
                if phase % CHUNK == 0:
                    arrived(dve, x_loaded, c, phase)
                for j in range(GROUP):
                    k = phase % CHUNK * GROUP + j
                    last = nc.vector.bn_stats(stats[:, p, k, :], x_all[:, bass.ds(g * GC + j * D, D)])
                if phase % CHUNK == CHUNK - 1:
                    last.then_inc(stat_step, 1)
                    st = stats[:, p, :, :]
                    dve.wait_ge(stat_step, c * 3 + 1)
                    nc.vector.scalar_tensor_tensor(out=sum_neg[:, :], in0=st[:, :, 1], scalar=-1.0,
                                                   in1=st[:, :, 4], op0=ALU.mult, op1=ALU.subtract)
                    nc.vector.tensor_tensor(squares[:, :], st[:, :, 2], st[:, :, 5], ALU.add)
                    nc.vector.tensor_tensor(diff[:, :], st[:, :, 1], st[:, :, 4], ALU.subtract
                                            ).then_inc(stat_step, 1)
                    dve.wait_ge(stat_step, c * 3 + 2)
                    nc.vector.tensor_tensor(diff_sq[:, :], diff[:, :], diff[:, :], ALU.mult
                                            ).then_inc(stat_step, 1)
                    if late(g, 2 * CHUNK):
                        dve.wait_ge(coef_ready, c - 1)
                    nc.vector.tensor_scalar(mean_neg[:, p, :], sum_neg[:, :], 0.5, None, ALU.mult)
                    dve.wait_ge(stat_step, c * 3 + 3)
                    nc.vector.scalar_tensor_tensor(out=var4[:, :], in0=squares[:, :], scalar=4.0 / D,
                                                   in1=diff_sq[:, :], op0=ALU.mult, op1=ALU.add
                                                   ).then_inc(var_step, 1)
                    dve.wait_ge(var_step, c + 1)
                    nc.vector.tensor_scalar(var_eps[:, p, :], var4[:, :], 0.25, EPS, ALU.mult, ALU.add
                                            ).then_inc(stats_ready, 1)

            def messages(g, phase):
                s = phase % 2
                dve.wait_ge(gate_ready, g + 1)
                if late(g):
                    dve.wait_ge(summed, g - 1)
                nc.vector.tensor_tensor(per_graph(vals[:, s, :]), prod_ps[s][:, :, 0, :],
                                        per_graph(gate[:, s, :]), ALU.mult).then_inc(vals_ready, 1)

            def low_part(g, phase):
                s = phase % 2
                dve.wait_ge(hi_ready, g + 1)
                if late(g):
                    dve.wait_ge(prod_ready, g - 1)
                nc.vector.scalar_tensor_tensor(out=hT_lo[:, s, :], in0=hT_ps[s], scalar=0.0,
                                               in1=hT_hi[:, s, :].bitcast(FP32), op0=ALU.max,
                                               op1=ALU.subtract).then_inc(hT_ready, 1)

            def output(g, phase):
                s = phase % 2
                dve.wait_ge(summed, g + 1)
                cols = x_all[:, bass.ds(g * GC, GC)]
                nc.vector.scalar_tensor_tensor(out=cols, in0=agg_ps[s], scalar=0.0, in1=cols,
                                               op0=ALU.max, op1=ALU.add).then_inc(out_ready, 1)

            def prepare():
                dve.wait_ge(w_turned, 1)
                nc.vector.tensor_copy(w_loop[:, 0, :], bank[6][:, 0:128])
                nc.vector.tensor_copy(w_gT[:, :], bank[6][:, 128:256]).then_inc(w_copied, 1)
                dve.wait_ge(w_turned, 2)
                nc.vector.tensor_copy(w_loop[:, 1, :], bank[7][:, 0:128]).then_inc(w_copied, 1)

                dve.wait_ge(w_copied, 2)
                w_both = w_loop[:, :, :].rearrange("p a d -> p (a d)")
                nc.vector.tensor_copy(w_hi[:, :], w_both).then_inc(w_copied, 1)
                dve.wait_ge(w_copied, 3)
                nc.vector.tensor_tensor(w_lo[:, :], w_both, w_hi[:, :].bitcast(FP32), ALU.subtract
                                        ).then_inc(w_split, 1)

                dve.wait_ge(bias_loaded, 32)
                b_row = bias_in[:, :, :].rearrange("p a d -> p (a d)")
                nc.vector.tensor_copy(part[0][:, :], b_row).then_inc(bias_step, 1)
                dve.wait_ge(bias_step, 2)
                nc.vector.tensor_tensor(rest[0][:, :], b_row, part[0][:, :], ALU.subtract).then_inc(bias_step, 1)
                dve.wait_ge(bias_step, 3)
                nc.vector.tensor_copy(part[1][:, :], rest[0][:, :]).then_inc(bias_step, 1)
                dve.wait_ge(bias_step, 4)
                nc.vector.tensor_tensor(rest[1][:, :], rest[0][:, :], part[1][:, :], ALU.subtract
                                        ).then_inc(bias_step, 1)
                dve.wait_ge(bias_step, 5)
                nc.vector.tensor_copy(part[2][:, :], rest[1][:, :]).then_inc(bias_step, 1)
                dve.wait_ge(const_ready, 4)
                nc.vector.tensor_scalar(mix[0][:, :], part[0][:, :], ident[0:3, 0:1], None, ALU.mult
                                        ).then_inc(bias_step, 1)
                dve.wait_ge(bias_step, 7)
                nc.vector.scalar_tensor_tensor(out=mix[1][:, :], in0=part[1][:, :], scalar=ident[0:3, 1:2],
                                               in1=mix[0][:, :], op0=ALU.mult, op1=ALU.add).then_inc(bias_step, 1)
                dve.wait_ge(bias_step, 8)
                nc.vector.scalar_tensor_tensor(out=mix[0][:, :], in0=part[2][:, :], scalar=ident[0:3, 2:3],
                                               in1=mix[1][:, :], op0=ALU.mult, op1=ALU.add).then_inc(bias_step, 1)
                dve.wait_ge(bias_step, 9)
                for j in range(2):
                    nc.vector.tensor_copy(bias_rows[0:3, j, :], mix[0][:, :]).then_inc(bias_step, 1)

            def step(t, c, phase):
                if isinstance(t, int) and t == -STATS + CHUNK:
                    prepare()
                if live(t):
                    messages(t, phase)
                if live(t - 1):
                    output(t - 1, (phase - 1) % UNROLL)
                if live(t + HT):
                    low_part(t + HT, (phase + HT) % UNROLL)
                if live(t + STATS):
                    row_stats(t + STATS, chunk_after(c, phase, STATS), (phase + STATS) % UNROLL)

            steps(dve, step, -STATS, GROUPS + 1)

            dve.wait_ge(dist_total, 1)
            nc.vector.reduce_sum(dist_sum[:, :], bank[0][0:1, 0:CHUNKS], axis=AX.X).then_inc(flag_step, 1)
            dve.wait_ge(flag_step, 1)
            nc.vector.tensor_scalar(flag[:, :], dist_sum[:, :], 0.5 * B * N * N, None, ALU.is_gt).then_inc(flag_ready, 1)

            dve.wait_ge(flag_ready, 1)
            with dve.If(dve.value_load(flag[0:1, 0:1], min_val=0, max_val=1) != 0):
                dve.wait_ge(stored, 16 * CHUNKS)
                dve.wait_ge(rel_made, 1)
                nc.vector.tensor_copy(rel_id[:, :], rel_int[:, :]).then_inc(g_summed, 1)
                nc.vector.tensor_copy(g_W[:, 2 * D:3 * D], w_loop[:, 0, :]).then_inc(g_summed, 1)
                nc.vector.tensor_copy(g_C[:, 2 * D:3 * D], w_loop[:, 1, :]).then_inc(g_out_ready, 1)
                for d in range(2):
                    dve.wait_ge(g_w_turned, 2 * d + 1)
                    nc.vector.tensor_copy(g_W[:, d * D:d * D + D], bank[6][:, 0:128])
                    nc.vector.tensor_copy(g_wgT[:, d * D:d * D + D], bank[6][:, 128:256]
                                          ).then_inc(g_setup, 1)
                    dve.wait_ge(g_w_turned, 2 * d + 2)
                    nc.vector.tensor_copy(g_C[:, d * D:d * D + D], bank[7][:, 0:128]).then_inc(g_setup, 1)
                dve.wait_ge(tab_loaded, 16 * 10)

                def wide(ap, n):
                    return ap.unsqueeze(1).to_broadcast([128, n, D])

                def blocks(ap, n):
                    return ap.rearrange("p (r d) -> p r d", r=n)

                with dve.Fori(0, B) as b:
                    dve.wait_ge(g_loaded, b * 32 + 32)
                    nc.vector.bn_stats(g_stats[:, :], g_x).then_inc(g_stat_step, 1)
                    dve.wait_ge(g_stat_step, b * 3 + 1)
                    nc.vector.tensor_copy(g_adjf, g_adj[:, :])
                    nc.vector.bn_aggr(g_moments[:, :], g_stats[:, :]).then_inc(g_stat_step, 1)
                    dve.wait_ge(g_stat_step, b * 3 + 2)
                    nc.vector.tensor_scalar(g_var[:, :], g_moments[:, 1:2], EPS, None, ALU.add
                                            ).then_inc(g_stat_step, 1)
                    dve.wait_ge(g_rstd_ready, b + 1)
                    nc.vector.tensor_scalar(g_xn, g_x, g_moments[:, 0:1], g_rstd[:, 0:1],
                                            ALU.subtract, ALU.mult).then_inc(g_normed, 1)

                    dve.wait_ge(g_PG, b + 1)
                    nc.vector.tensor_tensor(g_gatein[2], g_G[:, 2 * D:3 * D], bg_loop_tab, ALU.add
                                            ).then_inc(l_in_ready, 1)
                    nc.vector.tensor_scalar(g_mask[2], g_adjf, 1.0, None, ALU.is_equal)
                    nc.vector.tensor_tensor(g_vals[2], g_P[:, 2 * D:3 * D], b_loop_tab, ALU.add
                                            ).then_inc(l_val_step, 1)
                    dve.wait_ge(l_val_step, b + 1)
                    dve.wait_ge(l_gate_ready, b + 1)
                    nc.vector.tensor_tensor(g_vals[2], g_vals[2], g_gate[2], ALU.mult
                                            ).then_inc(l_vals_ready, 1)

                    with dve.Fori(0, BLOCKS) as k:
                        for d in range(2):
                            nc.vector.tensor_tensor(
                                blocks(g_gatein[d], REL_BLOCK), wide(g_G[:, d * D:d * D + D], REL_BLOCK),
                                blocks(bg_tab[d][:, bass.ds(k * RB, RB)], REL_BLOCK), ALU.add
                            ).then_inc(g_in_ready, 1)
                        for d in range(2):
                            dve.wait_ge(g_summed, b * UNITS + k * 2 + (d + 1))
                            nc.vector.tensor_tensor(
                                blocks(g_mask[d], REL_BLOCK), wide((g_adjT, g_adjf)[d], REL_BLOCK),
                                rel_id[:, bass.ds(k * REL_BLOCK, REL_BLOCK)].unsqueeze(2)
                                .to_broadcast([128, REL_BLOCK, N]), ALU.is_equal)
                            nc.vector.tensor_tensor(
                                blocks(g_vals[d], REL_BLOCK), wide(g_P[:, d * D:d * D + D], REL_BLOCK),
                                blocks(b_tab[d][:, bass.ds(k * RB, RB)], REL_BLOCK), ALU.add
                            ).then_inc(g_val_step, 1)
                            dve.wait_ge(g_val_step, b * UNITS + k * 2 + (d + 1))
                            dve.wait_ge(g_gate_ready, b * UNITS + k * 2 + (d + 1))
                            nc.vector.tensor_tensor(g_vals[d], g_vals[d], g_gate[d], ALU.mult
                                                    ).then_inc(g_vals_ready, 1)

                    dve.wait_ge(g_summed, b * UNITS + (UNITS + 2))
                    nc.vector.scalar_tensor_tensor(out=g_out, in0=bank[4][:, 0:D], scalar=0.0, in1=g_x,
                                                   op0=ALU.max, op1=ALU.add).then_inc(g_out_ready, 1)

        @block.tensor
        def _(pe):
            def turn_weights(raw_w, raw_g, gT, ready, copied, at):
                nc.tensor.transpose(bank[6][:, 0:128], raw_w, ident[:, :])
                nc.tensor.transpose(bank[6][:, 128:256], raw_g, ident[:, :]).then_inc(ready, 1)
                pe.wait_ge(copied, at)
                nc.tensor.matmul(bank[7][:, 0:128], raw_w, gT, start=True, stop=True).then_inc(ready, 1)

            pe.wait_ge(const_ready, 4)
            pe.wait_ge(w_loaded, 32)
            turn_weights(w_raw[:, 0, :], w_raw[:, 1, :], w_gT[:, :], w_turned, w_copied, 1)

            def turn_rows(g, phase):
                s = phase % 2
                pe.wait_ge(normed, g + 1)
                if late(g):
                    pe.wait_ge(hT_ready, g - 1)
                for j in range(GROUP):
                    last = nc.tensor.transpose(hT_ps[s][:, j * N:j * N + N], xn[:, s, j * D:j * D + D],
                                               ident[:, :])
                last.then_inc(turned, 1)

            def products(g, phase):
                s = phase % 2
                pe.wait_ge(hT_ready, g + 1)
                if late(g):
                    pe.wait_ge(vals_ready, g - 1)
                for q in range(0, GROUP, 2):
                    nc.tensor.matmul(prod_ps[s][:, q:q + 2, :, :], ones_b[:, :], bias_rows[:, :, :],
                                     start=True, stop=False)
                    for j in (q, q + 1):
                        hi, lo = (h[:, s, j * N:j * N + N] for h in (hT_hi, hT_lo))
                        to = prod_ps[s][:, j, :, :]
                        nc.tensor.matmul(to, hi, w_hi[:, :], start=False, stop=False)
                        nc.tensor.matmul(to, hi, w_lo[:, :], start=False, stop=False)
                        last = nc.tensor.matmul(to, lo, w_hi[:, :], start=False, stop=(j == q + 1))
                last.then_inc(prod_ready, 1)

            def aggregate(g, phase):
                s = phase % 2
                pe.wait_ge(mask_ready, g + 1)
                pe.wait_ge(vals_ready, g + 1)
                if late(g):
                    pe.wait_ge(out_ready, g - 1)
                for j in range(GROUP):
                    last = nc.tensor.matmul(agg_ps[s][:, j * D:j * D + D], mask[:, s, j * N:j * N + N],
                                            vals[:, s, j * D:j * D + D], start=True, stop=True)
                last.then_inc(summed, 1)

            def step(t, c, phase):
                if live(t + HT):
                    turn_rows(t + HT, (phase + HT) % UNROLL)
                if live(t + PROD):
                    if isinstance(t, int) and t == -PROD:
                        pe.wait_ge(w_split, 1)
                        pe.wait_ge(bias_step, 11)
                    products(t + PROD, (phase + PROD) % UNROLL)
                if live(t):
                    aggregate(t, phase)

            steps(pe, step, -HT, GROUPS)

            pe.wait_ge(dist_ready, CHUNKS)
            pe.wait_ge(hT_ready, GROUPS)
            nc.tensor.matmul(bank[0][0:1, 0:CHUNKS], ones[:, :], dist[:, :], start=True, stop=True
                             ).then_inc(dist_total, 1)

            pe.wait_ge(flag_ready, 1)
            with pe.If(pe.value_load(flag[0:1, 0:1], min_val=0, max_val=1) != 0):
                pe.wait_ge(tab_loaded, 16 * 10)
                for d in range(2):
                    if d:
                        pe.wait_ge(g_setup, 2)
                    turn_weights(g_wraw[:, 2 * d * D:2 * d * D + D],
                                 g_wraw[:, 2 * d * D + D:2 * d * D + 2 * D],
                                 g_wgT[:, d * D:d * D + D], g_w_turned, g_setup, 2 * d + 1)
                pe.wait_ge(g_setup, 4)
                with pe.Fori(0, B) as b:
                    pe.wait_ge(g_normed, b + 1)
                    nc.tensor.transpose(bank[0][:, 0:N], g_xn, ident[:, :])
                    nc.tensor.transpose(bank[1][:, 0:N], g_adjf, ident[:, :]).then_inc(g_turned, 1)
                    pe.wait_ge(g_hT_ready, b + 1)
                    nc.tensor.matmul(bank[2][:, 0:3 * D], g_hT, g_W, start=True, stop=True)
                    nc.tensor.matmul(bank[3][:, 0:3 * D], g_hT, g_C, start=True, stop=True
                                     ).then_inc(g_prod, 1)
                    pe.wait_ge(l_vals_ready, b + 1)
                    pe.wait_ge(g_out_ready, b + 1)
                    nc.tensor.matmul(bank[4][:, 0:D], g_mask[2], g_vals[2], start=True, stop=False,
                                     skip_group_check=True)
                    with pe.Fori(0, BLOCKS) as k:
                        for d in range(2):
                            pe.wait_ge(g_vals_ready, b * UNITS + k * 2 + (d + 1))
                            for r in range(REL_BLOCK):
                                last = nc.tensor.matmul(bank[4][:, 0:D], g_mask[d][:, r * N:r * N + N],
                                                        g_vals[d][:, r * D:r * D + D], start=False,
                                                        stop=False, skip_group_check=True)
                            last.then_inc(g_summed, 1)


_INS = ["x", "adj", "L0_gnn_W_fwd", "L0_gnn_W_bwd", "L0_gnn_W_loop", "L0_gnn_Wg_fwd", "L0_gnn_Wg_bwd",
        "L0_gnn_Wg_loop", "L0_gnn_b_fwd", "L0_gnn_b_bwd", "L0_gnn_b_loop", "L0_gnn_bg_fwd",
        "L0_gnn_bg_bwd", "L0_gnn_bg_loop"]


def kernel(**inputs):
    import concourse.bacc as bacc
    from concourse.bass_utils import run_bass_kernel_spmd

    nc = bacc.Bacc("TRN2", target_bir_lowering=False, num_devices=1)
    arrays, args = {}, []
    for name in _INS:
        a = np.ascontiguousarray(inputs[name])
        arrays[f"in_{name}"] = a
        args.append(nc.dram_tensor(f"in_{name}", a.shape, mybir.dt.from_np(a.dtype), kind="ExternalInput").ap())
    out = nc.dram_tensor("out", arrays["in_x"].shape, FP32, kind="ExternalOutput").ap()
    build(nc, *args, out)
    r = run_bass_kernel_spmd(nc, [arrays], core_ids=[0])
    return r.results[0]["out"]
```

```python
from contextlib import ExitStack

import numpy as np
import concourse.bass as bass
from concourse import mybir

FP32, FP32R, BF16, INT32 = mybir.dt.float32, mybir.dt.float32r, mybir.dt.bfloat16, mybir.dt.int32
ALU = mybir.AluOpType
ACT = mybir.ActivationFunctionType
AX = mybir.AxisListType

EPS = 1e-5
GROUP = 4
CHUNK = 2
UNROLL = 4
MASKS = 4
REL_BLOCK = 3


def build(nc, x, adj, W_fwd, W_bwd, W_loop, Wg_fwd, Wg_bwd, Wg_loop,
          b_fwd, b_bwd, b_loop, bg_fwd, bg_bwd, bg_loop, out):
    B, N, D = x.shape
    NREL = b_fwd.shape[0]
    assert N == 128 and D == 128 and B % (GROUP * CHUNK) == 0 and NREL % REL_BLOCK == 0
    GROUPS = B // GROUP
    CHUNKS = GROUPS // CHUNK
    GC = GROUP * D
    CG = GROUP * CHUNK
    CC = CG * D
    STORES = CHUNKS - 1 + CHUNK

    STATS, COEF, NORM, HT, PROD, MASK = 6, 4, 3, 2, 1, 1
    FILL_TO = -1
    LOOP_FROM = 4
    LOOP_TO = LOOP_FROM + (GROUPS - STATS - LOOP_FROM) // UNROLL * UNROLL
    assert LOOP_TO > LOOP_FROM
    LOAD_AHEAD = 8

    ctx = ExitStack()
    with ctx:
        def sb(name, shape, dt=FP32):
            return ctx.enter_context(nc.sbuf_tensor(name, shape, dt))

        def sem(name):
            return ctx.enter_context(nc.semaphore(name))

        SIDE = max(B * D, 2 * NREL * D + 36 * D)
        x_all = sb("x_all", [128, SIDE])
        adj_all = sb("adj_all", [128, SIDE], INT32)
        xn = sb("xn", [128, 2, GC])
        hT_hi = sb("hT_hi", [128, 2, GC], FP32R)
        hT_lo = sb("hT_lo", [128, 2, GC], FP32R)
        gate = sb("gate", [128, 2, GC])
        vals = sb("vals", [128, 2, GC])
        mask = sb("mask", [128, MASKS, GROUP * N])
        stats = sb("stats", [128, 2, CG, 6])
        sum_neg = sb("sum_neg", [128, CG])
        diff = sb("diff", [128, CG])
        diff_sq = sb("diff_sq", [128, CG])
        squares = sb("squares", [128, CG])
        var4 = sb("var4", [128, CG])
        mean_neg = sb("mean_neg", [128, 2, CG])
        var_eps = sb("var_eps", [128, 2, CG])
        rstd = sb("rstd", [128, 2, CG])
        shift = sb("shift", [128, 2, CG])
        minus_half = sb("minus_half", [128, CG])
        ident = sb("ident", [128, 128])
        ones = sb("ones", [128, 128])
        w_raw = sb("w_raw", [128, 2, 128])
        w_gT = sb("w_gT", [128, 128])
        w_hi = sb("w_hi", [128, 2 * D], FP32R)
        w_lo = sb("w_lo", [128, 2 * D], FP32R)
        ones_r = sb("ones_r", [128, 128], FP32R)
        bias_rows = sb("bias_rows", [128, 2, 2 * D], FP32R)
        bias_in = sb("bias_in", [2, 2, D])
        bias_hi = sb("bias_hi", [2, 2 * D], FP32R)
        past = sb("past", [2, 1])
        zeros = sb("zeros", [128, 4 * D])
        junk = sb("junk", [128, 2, CC], BF16)
        dist = sb("dist", [128, CHUNKS])
        dist_sum = sb("dist_sum", [1, 1])
        flag = sb("flag", [1, 1], INT32)

        psum = ctx.enter_context(nc.psum_tensor("psum", [128, 8 * 512], FP32))
        bank = [psum[:, n * 512:n * 512 + 512] for n in range(8)]
        hT_ps, agg_ps = bank[0:2], bank[6:8]
        end_ps = bank[1]
        prod_ps = [psum[:, n * 1024:n * 1024 + 1024].rearrange("p (g a d) -> p g a d", g=GROUP, a=2)
                   for n in (1, 2)]

        x_loaded = [sem(f"x_loaded{n}") for n in range(2)]
        adj_loaded = [sem(f"adj_loaded{n}") for n in range(2)]
        x_first = sem("x_first")
        w_loaded = sem("w_loaded")
        bias_loaded = sem("bias_loaded")
        half_ready = sem("half_ready")
        past_step = sem("past_step")
        ident_step = sem("ident_step")
        w_turned = sem("w_turned")
        w_gT_ready = sem("w_gT_ready")
        w_hi_ready = sem("w_hi_ready")
        w_lo_ready = sem("w_lo_ready")
        bias_hi_ready = sem("bias_hi_ready")
        ones_ready = sem("ones_ready")
        bias_step = sem("bias_step")
        first_step = sem("first_step")
        first_stats = sem("first_stats")
        first_rstd = sem("first_rstd")
        first_coef = sem("first_coef")
        stat_step = sem("stat_step")
        stats_ready = sem("stats_ready")
        rstd_ready = sem("rstd_ready")
        coef_ready = sem("coef_ready")
        normed = sem("normed")
        turned = sem("turned")
        hi_ready = sem("hi_ready")
        hT_ready = sem("hT_ready")
        prod_ready = sem("prod_ready")
        gate_ready = sem("gate_ready")
        vals_ready = sem("vals_ready")
        mask_ready = sem("mask_ready")
        summed = sem("summed")
        out_ready = sem("out_ready")
        stored = sem("stored")
        half_prod = sem("half_prod")
        half_gate = sem("half_gate")
        half_vals = sem("half_vals")
        half_summed = sem("half_summed")
        dist_ready = sem("dist_ready")
        dist_total = sem("dist_total")
        flag_step = sem("flag_step")
        flag_ready = sem("flag_ready")

        adj_f32 = adj_all[:, :].bitcast(FP32)
        TABLE = NREL * D
        room = {"x": 0, "a": 0}

        def view(side, cols):
            base = x_all[:, :] if side == "x" else adj_f32
            at = room[side]
            room[side] += cols
            assert room[side] <= SIDE
            return base[:, at:at + cols]

        DIRS = (("fwd", W_fwd, Wg_fwd), ("bwd", W_bwd, Wg_bwd))
        b_tab = [view("x", TABLE) for _ in DIRS]
        bg_tab = [view("a", TABLE) for _ in DIRS]
        RB = REL_BLOCK * D
        g_x, g_xn, g_hT, g_adjf, g_adjT, g_out = (view("x", D) for _ in range(6))
        g_vals = [view("x", RB) for _ in range(2)] + [view("x", D)]
        g_P = view("x", 3 * D)
        b_loop_tab = view("x", D)
        g_W = view("x", 3 * D)
        g_gatein = [view("a", RB) for _ in range(2)] + [view("a", D)]
        g_gate = [view("a", RB) for _ in range(2)] + [view("a", D)]
        g_mask = [view("a", RB) for _ in range(2)] + [view("a", D)]
        g_G = view("a", 3 * D)
        bg_loop_tab = view("a", D)
        g_C = view("a", 3 * D)
        g_wraw = view("a", 4 * D)
        g_wgT = view("a", 2 * D)
        g_adj = sb("g_adj", [128, N], INT32)
        g_stats = sb("g_stats", [128, 6])
        g_moments = sb("g_moments", [128, 2])
        g_var = sb("g_var", [128, 1])
        g_rstd = sb("g_rstd", [128, 1])
        rel_int = sb("rel_int", [128, NREL], INT32)
        rel_id = sb("rel_id", [128, NREL])
        BLOCKS = NREL // REL_BLOCK
        UNITS = 2 * BLOCKS

        tab_loaded = sem("tab_loaded")
        rel_made = sem("rel_made")
        g_setup = sem("g_setup")
        g_w_turned = sem("g_w_turned")
        g_loaded = sem("g_loaded")
        g_stat_step = sem("g_stat_step")
        g_rstd_ready = sem("g_rstd_ready")
        g_normed = sem("g_normed")
        g_turned = sem("g_turned")
        g_hT_ready = sem("g_hT_ready")
        g_prod = sem("g_prod")
        g_PG = sem("g_PG")
        g_in_ready = sem("g_in_ready")
        g_gate_ready = sem("g_gate_ready")
        g_val_step = sem("g_val_step")
        g_vals_ready = sem("g_vals_ready")
        g_summed = sem("g_summed")
        l_in_ready = sem("l_in_ready")
        l_gate_ready = sem("l_gate_ready")
        l_val_step = sem("l_val_step")
        l_vals_ready = sem("l_vals_ready")
        g_out_ready = sem("g_out_ready")
        g_stored = sem("g_stored")

        def per_graph(ap):
            return ap.rearrange("p (g d) -> p g d", g=GROUP)

        def live(g):
            return not isinstance(g, int) or 0 <= g < GROUPS

        def late(g, slots=2):
            return not isinstance(g, int) or g >= slots

        def steps(eng, step, first, last):
            for t in range(first, LOOP_FROM):
                step(t, t // CHUNK, t % UNROLL)
            with eng.Fori(LOOP_FROM // CHUNK, (LOOP_TO - UNROLL) // CHUNK + 1, UNROLL // CHUNK) as c:
                for j in range(UNROLL):
                    step(c * CHUNK + j, c + j // CHUNK, (LOOP_FROM + j) % UNROLL)
            for t in range(LOOP_TO, last):
                step(t, t // CHUNK, t % UNROLL)

        def filling(t):
            return isinstance(t, int) and t < FILL_TO

        def is_number(g, n):
            return isinstance(g, int) and g == n

        def parts(g):
            if is_number(g, GROUPS - 1):
                return (range(0, GROUP // 2), True), (range(GROUP // 2, GROUP), False)
            return (range(GROUP), False),

        def chunk_after(c, phase, ahead):
            return c + (phase % CHUNK + ahead) // CHUNK

        def arrived(eng, loaded, c, phase):
            p = phase // CHUNK % 2
            eng.wait_ge(loaded[p], (c - p) * 8 + 16)

        block = ctx.enter_context(nc.Block())

        @block.sync
        def _(sp):
            def load_tile(to, source, at, col, graphs, loaded):
                sp.dma_start(to[:, bass.ds(col, graphs * D)].rearrange("p (b d) -> p b d", b=graphs),
                             source[bass.ds(at, graphs), :, :].rearrange("b n d -> n b d")
                             ).then_inc(loaded, 16)

            def store_tile(at, col, graphs):
                sp.dma_start(out[bass.ds(at, graphs), :, :].rearrange("b n d -> n b d"),
                             x_all[:, bass.ds(col, graphs * D)].rearrange("p (b d) -> p b d", b=graphs)
                             ).then_inc(stored, 16)

            def places(c):
                if isinstance(c, int):
                    return c * CG, c * CC
                return sp.snap(c * CG), sp.snap(c * CC)

            def load(c, p):
                at, col = places(c)
                sp.wait_ge(x_loaded[p], (c - p) * 8)
                sp.wait_ge(adj_loaded[p], (c - p) * 8)
                load_tile(x_all, x, at, col, CG, x_loaded[p])
                load_tile(adj_all, adj, at, col, CG, adj_loaded[p])

            def store(c):
                at, col = places(c)
                sp.wait_ge(out_ready, c * CHUNK + CHUNK)
                store_tile(at, col, CG)

            ahead = min(LOAD_AHEAD, CHUNKS)
            load_tile(x_all, x, 0, 0, GROUP, x_first)
            load_tile(x_all, x, GROUP, GC, CG - GROUP, x_loaded[0])
            load_tile(x_all, x, CG, CC, CG, x_loaded[1])
            load_tile(adj_all, adj, 0, 0, CG, adj_loaded[0])
            load_tile(adj_all, adj, CG, CC, CG, adj_loaded[1])
            for c in range(2, ahead):
                load(c, c % 2)
            even = (CHUNKS - ahead) // 2 * 2
            if even:
                with sp.Fori(ahead, ahead + even - 1, 2) as c:
                    for j in range(2):
                        load(c + j, (ahead + j) % 2)
                        store(c + j - ahead)
            for c in range(even, CHUNKS - 1):
                store(c)
            for g in range(GROUPS - CHUNK, GROUPS):
                sp.wait_ge(out_ready, g + 1)
                store_tile(g * GROUP, g * GC, GROUP)
            sp.wait_ge(stored, 16 * STORES)

            sp.wait_ge(flag_ready, 1)
            with sp.If(sp.value_load(flag[0:1, 0:1], min_val=0, max_val=1) != 0):
                for d, (b_, bg_) in enumerate(((b_fwd, bg_fwd), (b_bwd, bg_bwd))):
                    sp.dma_start(b_tab[d], b_.rearrange("(o r) d -> o (r d)", o=1).to_broadcast([128, TABLE])
                                 ).then_inc(tab_loaded, 16)
                    sp.dma_start(bg_tab[d], bg_.rearrange("(o r) d -> o (r d)", o=1).to_broadcast([128, TABLE])
                                 ).then_inc(tab_loaded, 16)
                sp.dma_start(b_loop_tab, b_loop.to_broadcast([128, D])).then_inc(tab_loaded, 16)
                sp.dma_start(bg_loop_tab, bg_loop.to_broadcast([128, D])).then_inc(tab_loaded, 16)
                for d, (_, W, Wg) in enumerate(DIRS):
                    sp.dma_start(g_wraw[:, 2 * d * D:2 * d * D + D], W).then_inc(tab_loaded, 16)
                    sp.dma_start(g_wraw[:, 2 * d * D + D:2 * d * D + 2 * D], Wg).then_inc(tab_loaded, 16)
                sp.sem_inc(g_stored, 16)
                with sp.Fori(0, B) as b:
                    sp.wait_ge(g_stored, b * 16 + 16)
                    sp.dma_start(g_x, x[bass.ds(b, 1), :, :].rearrange("o n d -> n (o d)")
                                 ).then_inc(g_loaded, 16)
                    sp.dma_start(g_adj[:, :], adj[bass.ds(b, 1), :, :].rearrange("o n m -> n (o m)")
                                 ).then_inc(g_loaded, 16)
                    sp.wait_ge(g_out_ready, b + 2)
                    sp.dma_start(out[bass.ds(b, 1), :, :].rearrange("o n d -> n (o d)"), g_out
                                 ).then_inc(g_stored, 16)
                sp.wait_ge(g_stored, 16 * B + 16)

        @block.gpsimd
        def _(pool):
            pool.dma_start(bias_in[:, 0, :], b_loop.to_broadcast([2, D])).then_inc(bias_loaded, 16)
            pool.dma_start(bias_in[:, 1, :], bg_loop.to_broadcast([2, D])).then_inc(bias_loaded, 16)
            pool.memset(minus_half[:, :], -0.5).then_inc(half_ready, 1)
            pool.memset(past[:, :], -1.0).then_inc(past_step, 1)
            pool.memset(ident[:, :], 0.0).then_inc(ident_step, 1)
            pool.wait_ge(past_step, 1)
            pool.affine_select(out=past[:, :], in_=past[:, :], compare_op=ALU.is_ge, fill=0.0,
                               base=-1, pattern=[[-1, 1]], channel_multiplier=1).then_inc(past_step, 1)
            pool.wait_ge(ident_step, 1)
            pool.affine_select(out=ident[:, :], in_=ident[:, :], compare_op=ALU.not_equal, fill=1.0,
                               base=0, pattern=[[-1, 128]], channel_multiplier=1).then_inc(ident_step, 1)
            pool.wait_ge(half_ready, 1)

            def power(p, cols, ready, at, done):
                pool.tensor_tensor(rstd[:, p, cols], var_eps[:, p, cols], minus_half[:, cols], ALU.pow
                                   ).then_inc(ready, 1)
                pool.wait_ge(ready, at)
                pool.tensor_tensor(shift[:, p, cols], mean_neg[:, p, cols], rstd[:, p, cols], ALU.mult
                                   ).then_inc(done, 1)

            def coefficients(c, p):
                pool.wait_ge(stats_ready, c + 1)
                if not isinstance(c, int) or c >= 2:
                    pool.wait_ge(normed, c * CHUNK - CHUNK)
                power(p, slice(GROUP if is_number(c, 0) else 0, CG), rstd_ready, c + 1, coef_ready)

            def edges(g, c, phase):
                if phase % CHUNK == 0:
                    arrived(pool, adj_loaded, c, phase)
                if late(g, MASKS):
                    pool.wait_ge(summed, g - (MASKS - 1))
                pool.tensor_copy(mask[:, phase % MASKS, :], adj_all[:, bass.ds(g * GC, GC)]
                                 ).then_inc(mask_ready, 1)

            def step(t, c, phase):
                if live(t + MASK):
                    edges(t + MASK, chunk_after(c, phase, MASK), (phase + MASK) % UNROLL)
                if phase % CHUNK == 0 and live(t + COEF):
                    coefficients(chunk_after(c, phase, COEF), (phase + COEF) // CHUNK % 2)

            pool.wait_ge(first_stats, 1)
            power(0, slice(0, GROUP), first_rstd, 1, first_coef)
            steps(pool, step, -COEF, GROUPS)

            pool.wait_ge(flag_ready, 1)
            with pool.If(pool.value_load(flag[0:1, 0:1], min_val=0, max_val=1) != 0):
                pool.iota(rel_int[:, :], pattern=[[1, NREL]], base=2, channel_multiplier=0
                          ).then_inc(rel_made, 1)
                with pool.Fori(0, B) as b:
                    pool.wait_ge(g_stat_step, b * 3 + 3)
                    pool.tensor_tensor(g_rstd[:, :], g_var[:, :], minus_half[:, 0:1], ALU.pow
                                       ).then_inc(g_rstd_ready, 1)

        @block.scalar
        def _(act):
            act.preload_act_table(ACT.Sigmoid)
            act.dma_start(w_raw[:, 0, :], W_loop).then_inc(w_loaded, 16)
            act.dma_start(w_raw[:, 1, :], Wg_loop).then_inc(w_loaded, 16)

            def normalise(g, c, phase, graphs):
                s, p = phase % 2, phase // CHUNK % 2
                if graphs[0] == 0:
                    if is_number(g, 0):
                        act.wait_ge(first_coef, 1)
                    elif phase % CHUNK == 0 or is_number(g, 1):
                        act.wait_ge(coef_ready, c + 1)
                    if late(g):
                        act.wait_ge(turned, g - 1)
                for j in graphs:
                    k = phase % CHUNK * GROUP + j
                    last = nc.scalar.activation(
                        xn[:, s, j * D:j * D + D], x_all[:, bass.ds(g * GC + j * D, D)], ACT.Identity,
                        bias=shift[:, p, k:k + 1], scale=rstd[:, p, k:k + 1])
                if graphs[-1] == GROUP - 1:
                    last.then_inc(normed, 1)

            def relu_turned(g, phase):
                s = phase % 2
                act.wait_ge(turned, g + 1)
                if late(g):
                    act.wait_ge(prod_ready, g - 1)
                nc.scalar.activation(hT_hi[:, s, :], hT_ps[s], ACT.Relu).then_inc(hi_ready, 1)

            def sigmoid(g, phase):
                s = phase % 2
                for graphs, more in parts(g):
                    if more:
                        act.wait_ge(half_prod, 1)
                    else:
                        act.wait_ge(prod_ready, g + 1)
                    if late(g):
                        act.wait_ge(vals_ready, g - 1)
                    some = slice(graphs[0], graphs[-1] + 1)
                    nc.scalar.activation(per_graph(gate[:, s, :])[:, some, :], prod_ps[s][:, some, 1, :],
                                         ACT.Sigmoid).then_inc(half_gate if more else gate_ready, 1)

            def watch(c, phase):
                arrived(act, adj_loaded, c, phase)
                nc.scalar.activation(junk[:, phase // CHUNK % 2, :], adj_all[:, bass.ds(c * CC, CC)], ACT.Abs,
                                     bias=minus_half[:, 0:1],
                                     accum_out=dist[:, bass.ds(c, 1)]).then_inc(dist_ready, 1)

            def step(t, c, phase):
                norm = (t + NORM, chunk_after(c, phase, NORM), (phase + NORM) % UNROLL)
                if filling(t):
                    if live(t + NORM):
                        normalise(*norm, range(GROUP))
                    if live(t + HT):
                        relu_turned(t + HT, (phase + HT) % UNROLL)
                    return
                if live(t):
                    sigmoid(t, phase)
                if live(t + NORM):
                    normalise(*norm, range(0, GROUP // 2))
                if live(t + HT):
                    relu_turned(t + HT, (phase + HT) % UNROLL)
                if live(t + NORM):
                    normalise(*norm, range(GROUP // 2, GROUP))
                if (phase + 1) % CHUNK == 0 and live(t + 1):
                    watch(chunk_after(c, phase, 1), (phase + 1) % UNROLL)

            act.wait_ge(bias_loaded, 32)
            nc.scalar.activation(bias_hi[:, :], bias_in[:, :, :].rearrange("p a d -> p (a d)"), ACT.Copy
                                 ).then_inc(bias_hi_ready, 1)
            act.wait_ge(w_turned, 1)
            nc.scalar.activation(w_gT[:, :], bank[6][:, 128:256], ACT.Copy).then_inc(w_gT_ready, 1)
            nc.scalar.activation(w_hi[:, 0:D], bank[6][:, 0:D], ACT.Copy).then_inc(w_hi_ready, 1)
            act.wait_ge(w_turned, 2)
            nc.scalar.activation(w_hi[:, D:2 * D], bank[7][:, 0:D], ACT.Copy).then_inc(w_hi_ready, 1)
            act.wait_ge(half_ready, 1)
            steps(act, step, -NORM, GROUPS)

            act.wait_ge(flag_ready, 1)
            with act.If(act.value_load(flag[0:1, 0:1], min_val=0, max_val=1) != 0):
                with act.Fori(0, B) as b:
                    act.wait_ge(g_turned, b + 1)
                    nc.scalar.activation(g_hT, bank[0][:, 0:D], ACT.Relu)
                    nc.scalar.activation(g_adjT, bank[1][:, 0:N], ACT.Copy).then_inc(g_hT_ready, 1)
                    act.wait_ge(g_prod, b + 1)
                    nc.scalar.activation(g_P, bank[2][:, 0:3 * D], ACT.Copy)
                    nc.scalar.activation(g_G, bank[3][:, 0:3 * D], ACT.Copy).then_inc(g_PG, 1)
                    act.wait_ge(l_in_ready, b + 1)
                    nc.scalar.activation(g_gate[2], g_gatein[2], ACT.Sigmoid).then_inc(l_gate_ready, 1)
                    with act.Fori(0, BLOCKS) as k:
                        for d in range(2):
                            act.wait_ge(g_in_ready, b * UNITS + k * 2 + (d + 1))
                            nc.scalar.activation(g_gate[d], g_gatein[d], ACT.Sigmoid
                                                 ).then_inc(g_gate_ready, 1)

        @block.vector
        def _(dve):
            nc.vector.memset(ones[:, :], 1.0).then_inc(ones_ready, 1)
            nc.vector.memset(zeros[:, :], 0.0).then_inc(bias_step, 1)
            dve.wait_ge(ones_ready, 1)
            nc.vector.tensor_copy(ones_r[:, :], ones[:, :]).then_inc(ones_ready, 1)
            dve.wait_ge(bias_step, 1)
            nc.vector.tensor_copy(bias_rows[:, :, :].rearrange("p a d -> p (a d)"), zeros[:, :]
                                  ).then_inc(bias_step, 1)

            def row_stats(g, c, phase):
                p = phase // CHUNK % 2
                if is_number(g, 0):
                    dve.wait_ge(x_first, 16)
                elif phase % CHUNK == 0 or is_number(g, 1):
                    arrived(dve, x_loaded, c, phase)
                for j in range(GROUP):
                    k = phase % CHUNK * GROUP + j
                    last = nc.vector.bn_stats(stats[:, p, k, :], x_all[:, bass.ds(g * GC + j * D, D)])
                if is_number(g, 0):
                    last.then_inc(first_step, 1)
                elif phase % CHUNK == CHUNK - 1:
                    last.then_inc(stat_step, 1)

            def sums(p, cols, step, at):
                st = stats[:, p, cols, :]
                dve.wait_ge(step, at)
                nc.vector.scalar_tensor_tensor(out=sum_neg[:, cols], in0=st[:, :, 1], scalar=-1.0,
                                               in1=st[:, :, 4], op0=ALU.mult, op1=ALU.subtract)
                nc.vector.tensor_tensor(squares[:, cols], st[:, :, 2], st[:, :, 5], ALU.add)
                nc.vector.tensor_tensor(diff[:, cols], st[:, :, 1], st[:, :, 4], ALU.subtract
                                        ).then_inc(step, 1)

            def mean(p, cols, step, at):
                dve.wait_ge(step, at + 1)
                nc.vector.tensor_tensor(diff_sq[:, cols], diff[:, cols], diff[:, cols], ALU.mult
                                        ).then_inc(step, 1)
                nc.vector.tensor_scalar(mean_neg[:, p, cols], sum_neg[:, cols], 0.5, None, ALU.mult)

            def variance(p, cols, step, at):
                dve.wait_ge(step, at + 2)
                nc.vector.scalar_tensor_tensor(out=var4[:, cols], in0=squares[:, cols], scalar=4.0 / D,
                                               in1=diff_sq[:, cols], op0=ALU.mult, op1=ALU.add
                                               ).then_inc(step, 1)

            def variance_eps(p, cols, step, at, ready):
                dve.wait_ge(step, at + 3)
                nc.vector.tensor_scalar(var_eps[:, p, cols], var4[:, cols], 0.25, EPS, ALU.mult, ALU.add
                                        ).then_inc(ready, 1)

            def messages(g, phase):
                s = phase % 2
                for graphs, more in parts(g):
                    if more:
                        dve.wait_ge(half_gate, 1)
                    else:
                        dve.wait_ge(gate_ready, g + 1)
                    if late(g):
                        dve.wait_ge(summed, g - 1)
                    some = slice(graphs[0], graphs[-1] + 1)
                    nc.vector.tensor_tensor(per_graph(vals[:, s, :])[:, some, :], prod_ps[s][:, some, 0, :],
                                            per_graph(gate[:, s, :])[:, some, :], ALU.mult
                                            ).then_inc(half_vals if more else vals_ready, 1)

            def low_part(g, phase):
                s = phase % 2
                dve.wait_ge(hi_ready, g + 1)
                if late(g):
                    dve.wait_ge(prod_ready, g - 1)
                nc.vector.scalar_tensor_tensor(out=hT_lo[:, s, :], in0=hT_ps[s], scalar=0.0,
                                               in1=hT_hi[:, s, :].bitcast(FP32), op0=ALU.max,
                                               op1=ALU.subtract).then_inc(hT_ready, 1)

            def output(g, phase):
                s = phase % 2
                for graphs, more in parts(g):
                    if more:
                        dve.wait_ge(half_summed, 1)
                    else:
                        dve.wait_ge(summed, g + 1)
                    at, size = graphs[0] * D, len(graphs) * D
                    sums_ps = (end_ps if at else agg_ps[s])[:, at:at + size]
                    cols = x_all[:, bass.ds(g * GC + at, size)]
                    done = nc.vector.scalar_tensor_tensor(out=cols, in0=sums_ps, scalar=0.0, in1=cols,
                                                          op0=ALU.max, op1=ALU.add)
                    if not more:
                        done.then_inc(out_ready, 1)

            def split_bias():
                dve.wait_ge(past_step, 2)
                dve.wait_ge(bias_hi_ready, 1)
                dve.wait_ge(bias_step, 2)
                for n in range(2):
                    nc.vector.scalar_tensor_tensor(
                        out=bias_rows[0:2, n, :], in0=bias_hi[:, :].bitcast(FP32), scalar=past[:, 0:1],
                        in1=bias_in[:, :, :].rearrange("p a d -> p (a d)"), op0=ALU.mult, op1=ALU.add
                    ).then_inc(bias_step, 1)

            def split_weights():
                for n in range(2):
                    dve.wait_ge(w_hi_ready, n + 1)
                    nc.vector.tensor_tensor(w_lo[:, n * D:n * D + D], bank[6 + n][:, 0:D],
                                            w_hi[:, n * D:n * D + D].bitcast(FP32), ALU.subtract
                                            ).then_inc(w_lo_ready, 1)

            def step(t, c, phase):
                g, cg, ph = t + STATS, chunk_after(c, phase, STATS), (phase + STATS) % UNROLL
                p = ph // CHUNK % 2
                chunk_done = live(g) and ph % CHUNK == CHUNK - 1
                of = (p, slice(GROUP if is_number(cg, 0) else 0, CG), stat_step, cg * 4 + 1)

                if filling(t):
                    if live(t + HT):
                        low_part(t + HT, (phase + HT) % UNROLL)
                    row_stats(g, cg, ph)
                    if is_number(g, 0):
                        of = (0, slice(0, GROUP), first_step, 1)
                        sums(*of)
                        mean(*of)
                        variance(*of)
                        variance_eps(*of, first_stats)
                    elif chunk_done:
                        if cg >= 2:
                            dve.wait_ge(coef_ready, cg - 1)
                        sums(*of)
                        mean(*of)
                        variance(*of)
                        variance_eps(*of, stats_ready)
                    if t == -3:
                        split_weights()
                        split_bias()
                    return

                if live(g):
                    row_stats(g, cg, ph)
                if live(t):
                    messages(t, phase)
                if chunk_done:
                    sums(*of)
                if live(t - 1):
                    output(t - 1, (phase - 1) % UNROLL)
                if chunk_done:
                    dve.wait_ge(coef_ready, cg - 1)
                    mean(*of)
                    variance(*of)
                if live(t + HT):
                    low_part(t + HT, (phase + HT) % UNROLL)
                if chunk_done:
                    variance_eps(*of, stats_ready)

            steps(dve, step, -STATS, GROUPS + 1)

            dve.wait_ge(dist_total, 1)
            nc.vector.reduce_sum(dist_sum[:, :], bank[0][0:1, 0:CHUNKS], axis=AX.X).then_inc(flag_step, 1)
            dve.wait_ge(flag_step, 1)
            nc.vector.tensor_scalar(flag[:, :], dist_sum[:, :], 0.5 * B * N * N, None, ALU.is_gt).then_inc(flag_ready, 1)

            dve.wait_ge(flag_ready, 1)
            with dve.If(dve.value_load(flag[0:1, 0:1], min_val=0, max_val=1) != 0):
                dve.wait_ge(stored, 16 * STORES)
                dve.wait_ge(rel_made, 1)
                nc.vector.tensor_copy(rel_id[:, :], rel_int[:, :]).then_inc(g_summed, 1)
                for n, (to, ready) in enumerate(((g_W, g_summed), (g_C, g_out_ready))):
                    nc.vector.tensor_tensor(to[:, 2 * D:3 * D], w_hi[:, n * D:n * D + D].bitcast(FP32),
                                            w_lo[:, n * D:n * D + D].bitcast(FP32), ALU.add).then_inc(ready, 1)
                for d in range(2):
                    dve.wait_ge(g_w_turned, 2 * d + 1)
                    nc.vector.tensor_copy(g_W[:, d * D:d * D + D], bank[6][:, 0:128])
                    nc.vector.tensor_copy(g_wgT[:, d * D:d * D + D], bank[6][:, 128:256]
                                          ).then_inc(g_setup, 1)
                    dve.wait_ge(g_w_turned, 2 * d + 2)
                    nc.vector.tensor_copy(g_C[:, d * D:d * D + D], bank[7][:, 0:128]).then_inc(g_setup, 1)
                dve.wait_ge(tab_loaded, 16 * 10)

                def wide(ap, n):
                    return ap.unsqueeze(1).to_broadcast([128, n, D])

                def blocks(ap, n):
                    return ap.rearrange("p (r d) -> p r d", r=n)

                with dve.Fori(0, B) as b:
                    dve.wait_ge(g_loaded, b * 32 + 32)
                    nc.vector.bn_stats(g_stats[:, :], g_x).then_inc(g_stat_step, 1)
                    dve.wait_ge(g_stat_step, b * 3 + 1)
                    nc.vector.tensor_copy(g_adjf, g_adj[:, :])
                    nc.vector.bn_aggr(g_moments[:, :], g_stats[:, :]).then_inc(g_stat_step, 1)
                    dve.wait_ge(g_stat_step, b * 3 + 2)
                    nc.vector.tensor_scalar(g_var[:, :], g_moments[:, 1:2], EPS, None, ALU.add
                                            ).then_inc(g_stat_step, 1)
                    dve.wait_ge(g_rstd_ready, b + 1)
                    nc.vector.tensor_scalar(g_xn, g_x, g_moments[:, 0:1], g_rstd[:, 0:1],
                                            ALU.subtract, ALU.mult).then_inc(g_normed, 1)

                    dve.wait_ge(g_PG, b + 1)
                    nc.vector.tensor_tensor(g_gatein[2], g_G[:, 2 * D:3 * D], bg_loop_tab, ALU.add
                                            ).then_inc(l_in_ready, 1)
                    nc.vector.tensor_scalar(g_mask[2], g_adjf, 1.0, None, ALU.is_equal)
                    nc.vector.tensor_tensor(g_vals[2], g_P[:, 2 * D:3 * D], b_loop_tab, ALU.add
                                            ).then_inc(l_val_step, 1)
                    dve.wait_ge(l_val_step, b + 1)
                    dve.wait_ge(l_gate_ready, b + 1)
                    nc.vector.tensor_tensor(g_vals[2], g_vals[2], g_gate[2], ALU.mult
                                            ).then_inc(l_vals_ready, 1)

                    with dve.Fori(0, BLOCKS) as k:
                        for d in range(2):
                            nc.vector.tensor_tensor(
                                blocks(g_gatein[d], REL_BLOCK), wide(g_G[:, d * D:d * D + D], REL_BLOCK),
                                blocks(bg_tab[d][:, bass.ds(k * RB, RB)], REL_BLOCK), ALU.add
                            ).then_inc(g_in_ready, 1)
                        for d in range(2):
                            dve.wait_ge(g_summed, b * UNITS + k * 2 + (d + 1))
                            nc.vector.tensor_tensor(
                                blocks(g_mask[d], REL_BLOCK), wide((g_adjT, g_adjf)[d], REL_BLOCK),
                                rel_id[:, bass.ds(k * REL_BLOCK, REL_BLOCK)].unsqueeze(2)
                                .to_broadcast([128, REL_BLOCK, N]), ALU.is_equal)
                            nc.vector.tensor_tensor(
                                blocks(g_vals[d], REL_BLOCK), wide(g_P[:, d * D:d * D + D], REL_BLOCK),
                                blocks(b_tab[d][:, bass.ds(k * RB, RB)], REL_BLOCK), ALU.add
                            ).then_inc(g_val_step, 1)
                            dve.wait_ge(g_val_step, b * UNITS + k * 2 + (d + 1))
                            dve.wait_ge(g_gate_ready, b * UNITS + k * 2 + (d + 1))
                            nc.vector.tensor_tensor(g_vals[d], g_vals[d], g_gate[d], ALU.mult
                                                    ).then_inc(g_vals_ready, 1)

                    dve.wait_ge(g_summed, b * UNITS + (UNITS + 2))
                    nc.vector.scalar_tensor_tensor(out=g_out, in0=bank[4][:, 0:D], scalar=0.0, in1=g_x,
                                                   op0=ALU.max, op1=ALU.add).then_inc(g_out_ready, 1)

        @block.tensor
        def _(pe):
            def turn_weights(raw_w, raw_g, gT, ready, copied, at):
                nc.tensor.transpose(bank[6][:, 0:128], raw_w, ident[:, :])
                nc.tensor.transpose(bank[6][:, 128:256], raw_g, ident[:, :]).then_inc(ready, 1)
                pe.wait_ge(copied, at)
                nc.tensor.matmul(bank[7][:, 0:128], raw_w, gT, start=True, stop=True).then_inc(ready, 1)

            pe.wait_ge(ident_step, 2)
            pe.wait_ge(w_loaded, 32)
            turn_weights(w_raw[:, 0, :], w_raw[:, 1, :], w_gT[:, :], w_turned, w_gT_ready, 1)

            def turn_rows(g, phase):
                s = phase % 2
                pe.wait_ge(normed, g + 1)
                if late(g):
                    pe.wait_ge(hT_ready, g - 1)
                for j in range(GROUP):
                    last = nc.tensor.transpose(hT_ps[s][:, j * N:j * N + N], xn[:, s, j * D:j * D + D],
                                               ident[:, :])
                last.then_inc(turned, 1)

            def products(g, phase):
                s = phase % 2
                pe.wait_ge(hT_ready, g + 1)
                if late(g):
                    pe.wait_ge(vals_ready, g - 1)
                for q in range(0, GROUP, 2):
                    nc.tensor.matmul(prod_ps[s][:, q:q + 2, :, :], ones_r[:, :], bias_rows[:, :, :],
                                     start=True, stop=False)
                    for j in (q, q + 1):
                        hi, lo = (h[:, s, j * N:j * N + N] for h in (hT_hi, hT_lo))
                        to = prod_ps[s][:, j, :, :]
                        nc.tensor.matmul(to, hi, w_hi[:, :], start=False, stop=False)
                        nc.tensor.matmul(to, hi, w_lo[:, :], start=False, stop=False)
                        last = nc.tensor.matmul(to, lo, w_hi[:, :], start=False, stop=(j == q + 1))
                    if is_number(g, GROUPS - 1) and q == 0:
                        last.then_inc(half_prod, 1)
                last.then_inc(prod_ready, 1)

            def aggregate(g, phase):
                s = phase % 2
                pe.wait_ge(mask_ready, g + 1)
                for graphs, more in parts(g):
                    to = end_ps if graphs[0] else agg_ps[s]
                    if more:
                        pe.wait_ge(half_vals, 1)
                    else:
                        pe.wait_ge(vals_ready, g + 1)
                    if late(g) and not graphs[0]:
                        pe.wait_ge(out_ready, g - 1)
                    for j in graphs:
                        last = nc.tensor.matmul(to[:, j * D:j * D + D],
                                                mask[:, phase % MASKS, j * N:j * N + N],
                                                vals[:, s, j * D:j * D + D], start=True, stop=True)
                    last.then_inc(half_summed if more else summed, 1)

            def step(t, c, phase):
                if live(t + HT):
                    turn_rows(t + HT, (phase + HT) % UNROLL)
                if live(t + PROD):
                    if is_number(t, -PROD):
                        pe.wait_ge(w_lo_ready, 2)
                        pe.wait_ge(ones_ready, 2)
                        pe.wait_ge(bias_step, 4)
                    products(t + PROD, (phase + PROD) % UNROLL)
                if live(t):
                    aggregate(t, phase)

            steps(pe, step, -HT, GROUPS)

            pe.wait_ge(dist_ready, CHUNKS)
            pe.wait_ge(hT_ready, GROUPS)
            nc.tensor.matmul(bank[0][0:1, 0:CHUNKS], ones[:, 0:1], dist[:, :], start=True, stop=True
                             ).then_inc(dist_total, 1)

            pe.wait_ge(flag_ready, 1)
            with pe.If(pe.value_load(flag[0:1, 0:1], min_val=0, max_val=1) != 0):
                pe.wait_ge(tab_loaded, 16 * 10)
                for d in range(2):
                    if d:
                        pe.wait_ge(g_setup, 2)
                    turn_weights(g_wraw[:, 2 * d * D:2 * d * D + D],
                                 g_wraw[:, 2 * d * D + D:2 * d * D + 2 * D],
                                 g_wgT[:, d * D:d * D + D], g_w_turned, g_setup, 2 * d + 1)
                pe.wait_ge(g_setup, 4)
                with pe.Fori(0, B) as b:
                    pe.wait_ge(g_normed, b + 1)
                    nc.tensor.transpose(bank[0][:, 0:N], g_xn, ident[:, :])
                    nc.tensor.transpose(bank[1][:, 0:N], g_adjf, ident[:, :]).then_inc(g_turned, 1)
                    pe.wait_ge(g_hT_ready, b + 1)
                    nc.tensor.matmul(bank[2][:, 0:3 * D], g_hT, g_W, start=True, stop=True)
                    nc.tensor.matmul(bank[3][:, 0:3 * D], g_hT, g_C, start=True, stop=True
                                     ).then_inc(g_prod, 1)
                    pe.wait_ge(l_vals_ready, b + 1)
                    pe.wait_ge(g_out_ready, b + 1)
                    nc.tensor.matmul(bank[4][:, 0:D], g_mask[2], g_vals[2], start=True, stop=False,
                                     skip_group_check=True)
                    with pe.Fori(0, BLOCKS) as k:
                        for d in range(2):
                            pe.wait_ge(g_vals_ready, b * UNITS + k * 2 + (d + 1))
                            for r in range(REL_BLOCK):
                                last = nc.tensor.matmul(bank[4][:, 0:D], g_mask[d][:, r * N:r * N + N],
                                                        g_vals[d][:, r * D:r * D + D], start=False,
                                                        stop=False, skip_group_check=True)
                            last.then_inc(g_summed, 1)


_INS = ["x", "adj", "L0_gnn_W_fwd", "L0_gnn_W_bwd", "L0_gnn_W_loop", "L0_gnn_Wg_fwd", "L0_gnn_Wg_bwd",
        "L0_gnn_Wg_loop", "L0_gnn_b_fwd", "L0_gnn_b_bwd", "L0_gnn_b_loop", "L0_gnn_bg_fwd",
        "L0_gnn_bg_bwd", "L0_gnn_bg_loop"]


def kernel(**inputs):
    import concourse.bacc as bacc
    from concourse.bass_utils import run_bass_kernel_spmd

    nc = bacc.Bacc("TRN2", target_bir_lowering=False, num_devices=1)
    arrays, args = {}, []
    for name in _INS:
        a = np.ascontiguousarray(inputs[name])
        arrays[f"in_{name}"] = a
        args.append(nc.dram_tensor(f"in_{name}", a.shape, mybir.dt.from_np(a.dtype), kind="ExternalInput").ap())
    out = nc.dram_tensor("out", arrays["in_x"].shape, FP32, kind="ExternalOutput").ap()
    build(nc, *args, out)
    r = run_bass_kernel_spmd(nc, [arrays], core_ids=[0])
    return r.results[0]["out"]
```
